# Optimizing a Trainium2 kernel written in Bass

```python
import numpy as np
import jax
import jax.numpy as jnp

def _softmax(x, axis=-1):
    return jax.nn.softmax(x, axis=axis)

def _gelu(x):
    return jax.nn.gelu(x, approximate=True)

def _silu(x):
    return jax.nn.silu(x)

def _sigmoid(x):
    return jax.nn.sigmoid(x)

def _layernorm(x, axis=-1, eps=1e-05):
    m = jnp.mean(x, axis=axis, keepdims=True)
    v = jnp.var(x, axis=axis, keepdims=True)
    return (x - m) / jnp.sqrt(v + eps)

def _scatter_add(tgt, idx, src, axis=0):
    return tgt.at[idx].add(src)

def _segment_sum(src, seg, n):
    return jax.ops.segment_sum(src, seg, n)
kernel_name = 'mk_hybrid_d1_jaxref_r8_d1c295'

def setup_inputs(seed: int=0):
    np.random.seed(seed)
    _w = jnp.asarray

    def _L0_attn_a_setup():
        import jax, jax.numpy as jnp
        import numpy as np
        NUM_HEADS = 16
        key = jax.random.key(seed)
        ks = jax.random.split(key, 6)
        B, S, D = (2, 256, 128)
        x = jax.random.normal(ks[0], (B, S, D), dtype=jnp.float32)
        s = 1.0 / np.sqrt(D)
        Wq = jax.random.normal(ks[1], (D, D), dtype=jnp.float32) * s
        Wk = jax.random.normal(ks[2], (D, D), dtype=jnp.float32) * s
        Wv = jax.random.normal(ks[3], (D, D), dtype=jnp.float32) * s
        Wff = jax.random.normal(ks[4], (D, D), dtype=jnp.float32) * s
        bff = jax.random.normal(ks[5], (D,), dtype=jnp.float32) * 0.01
        return {'x': x, 'Wq': Wq, 'Wk': Wk, 'Wv': Wv, 'Wff': Wff, 'bff': bff}
    _L0_attn_a_in = _L0_attn_a_setup()

    def _L0_attn_b_setup():
        import jax, jax.numpy as jnp
        import numpy as np
        B, L, D, N = (2, 256, 128, 16)
        H = D // N
        THETA = 10000.0

        def apply_rope(x):
            l, h = (x.shape[-2], x.shape[-1])
            freqs = THETA ** (-jnp.arange(0, h, 2, dtype=jnp.float32) / h)
            ang = jnp.arange(l, dtype=jnp.float32)[:, None] * freqs
            cos, sin = (jnp.cos(ang), jnp.sin(ang))
            x_even = x[..., 0::2]
            x_odd = x[..., 1::2]
            out_even = cos * x_even - sin * x_odd
            out_odd = sin * x_even + cos * x_odd
            return jnp.stack((out_even, out_odd), axis=-1).reshape(x.shape)
        key = jax.random.key(seed)
        ks = jax.random.split(key, 9)
        s = 0.02
        return {'x': jax.random.normal(ks[0], (B, L, D), dtype=jnp.float32), 'Wq': jax.random.normal(ks[1], (D, D), dtype=jnp.float32) * s, 'bq': jax.random.normal(ks[2], (D,), dtype=jnp.float32) * s, 'Wk': jax.random.normal(ks[3], (D, D), dtype=jnp.float32) * s, 'bk': jax.random.normal(ks[4], (D,), dtype=jnp.float32) * s, 'Wv': jax.random.normal(ks[5], (D, D), dtype=jnp.float32) * s, 'bv': jax.random.normal(ks[6], (D,), dtype=jnp.float32) * s, 'Wo': jax.random.normal(ks[7], (D, D), dtype=jnp.float32) * s, 'bo': jax.random.normal(ks[8], (D,), dtype=jnp.float32) * s, 'scale': jnp.ones((1,), dtype=jnp.float32) * H ** (-0.5)}
    _L0_attn_b_in = _L0_attn_b_setup()

    def _L0_ffn_setup():
        import jax, jax.numpy as jnp
        import numpy as np
        NUM_EXPERTS = 8
        TOP_K = 2
        DIM = 128
        HIDDEN = 512
        B, S = (4, 256)
        key = jax.random.key(seed)
        ks = jax.random.split(key, 6)
        scale = 0.02
        x = jax.random.normal(ks[0], (B, S, DIM), dtype=jnp.float32)
        wg = jax.random.normal(ks[1], (NUM_EXPERTS, DIM), dtype=jnp.float32) * scale
        bg = jnp.zeros((NUM_EXPERTS,), dtype=jnp.float32)
        Wgate = jax.random.normal(ks[2], (NUM_EXPERTS, HIDDEN, DIM), dtype=jnp.float32) * scale
        Wup = jax.random.normal(ks[3], (NUM_EXPERTS, HIDDEN, DIM), dtype=jnp.float32) * scale
        Wdown = jax.random.normal(ks[4], (NUM_EXPERTS, DIM, HIDDEN), dtype=jnp.float32) * scale
        return {'x': x, 'wg': wg, 'bg': bg, 'Wgate': Wgate, 'Wup': Wup, 'Wdown': Wdown}
    _L0_ffn_in = _L0_ffn_setup()
    _d = {'L0_attn_a_x': _L0_attn_a_in['x'], 'L0_attn_a_Wq': _L0_attn_a_in['Wq'], 'L0_attn_a_Wk': _L0_attn_a_in['Wk'], 'L0_attn_a_Wv': _L0_attn_a_in['Wv'], 'L0_attn_a_Wff': _L0_attn_a_in['Wff'], 'L0_attn_a_bff': _L0_attn_a_in['bff'], 'L0_attn_b_Wq': _L0_attn_b_in['Wq'], 'L0_attn_b_bq': _L0_attn_b_in['bq'], 'L0_attn_b_Wk': _L0_attn_b_in['Wk'], 'L0_attn_b_bk': _L0_attn_b_in['bk'], 'L0_attn_b_Wv': _L0_attn_b_in['Wv'], 'L0_attn_b_bv': _L0_attn_b_in['bv'], 'L0_attn_b_Wo': _L0_attn_b_in['Wo'], 'L0_attn_b_bo': _L0_attn_b_in['bo'], 'L0_attn_b_scale': _L0_attn_b_in['scale'], 'L0_ffn_wg': _L0_ffn_in['wg'], 'L0_ffn_bg': _L0_ffn_in['bg'], 'L0_ffn_Wgate': _L0_ffn_in['Wgate'], 'L0_ffn_Wup': _L0_ffn_in['Wup'], 'L0_ffn_Wdown': _L0_ffn_in['Wdown']}
    _x0 = _d['L0_attn_a_x']
    _d['L0_attn_a_x'] = jax.random.normal(jax.random.fold_in(jax.random.key(seed), 1), (16, 256, 128), dtype=_x0.dtype)
    del _x0
    return _d

def reference(L0_attn_a_x, L0_attn_a_Wq, L0_attn_a_Wk, L0_attn_a_Wv, L0_attn_a_Wff, L0_attn_a_bff, L0_attn_b_Wq, L0_attn_b_bq, L0_attn_b_Wk, L0_attn_b_bk, L0_attn_b_Wv, L0_attn_b_bv, L0_attn_b_Wo, L0_attn_b_bo, L0_attn_b_scale, L0_ffn_wg, L0_ffn_bg, L0_ffn_Wgate, L0_ffn_Wup, L0_ffn_Wdown):

    def _L0_attn_a_ref(x, Wq, Wk, Wv, Wff, bff):
        import jax, jax.numpy as jnp
        import numpy as np
        NUM_HEADS = 16
        B, S, D = x.shape
        H = NUM_HEADS
        Dh = D // H
        q = x @ Wq.T * (1.0 / jnp.sqrt(jnp.asarray(D, x.dtype)))
        k = x @ Wk.T
        v = x @ Wv.T
        q = q.reshape(B, S, H, Dh)
        k = k.reshape(B, S, H, Dh)
        v = v.reshape(B, S, H, Dh)
        scores = jnp.einsum('bqhd,bkhd->bhqk', q, k)
        attn = jax.nn.softmax(scores, axis=-1)
        out = jnp.einsum('bhqk,bkhd->bqhd', attn, v).reshape(B, S, D)
        return out @ Wff.T + bff

    def _L0_attn_b_ref(x, Wq, bq, Wk, bk, Wv, bv, Wo, bo, scale):
        import jax, jax.numpy as jnp
        import numpy as np
        B, L, D, N = (2, 256, 128, 16)
        H = D // N
        THETA = 10000.0

        def apply_rope(x):
            l, h = (x.shape[-2], x.shape[-1])
            freqs = THETA ** (-jnp.arange(0, h, 2, dtype=jnp.float32) / h)
            ang = jnp.arange(l, dtype=jnp.float32)[:, None] * freqs
            cos, sin = (jnp.cos(ang), jnp.sin(ang))
            x_even = x[..., 0::2]
            x_odd = x[..., 1::2]
            out_even = cos * x_even - sin * x_odd
            out_odd = sin * x_even + cos * x_odd
            return jnp.stack((out_even, out_odd), axis=-1).reshape(x.shape)
        b, l, d = x.shape
        q = x @ Wq.T + bq
        k = x @ Wk.T + bk
        v = x @ Wv.T + bv
        q = q.reshape(b, l, N, H).transpose(0, 2, 1, 3)
        k = k.reshape(b, l, N, H).transpose(0, 2, 1, 3)
        v = v.reshape(b, l, N, H).transpose(0, 2, 1, 3)
        q = apply_rope(q) * scale
        k = apply_rope(k)
        dots = jnp.einsum('bnih,bnjh->bnij', q, k)
        i = jnp.arange(l)
        mask = i[:, None] < i[None, :]
        dots = jnp.where(mask, jnp.float32(-100000.0), dots)
        attn = jax.nn.softmax(dots, axis=-1)
        o = jnp.einsum('bnij,bnjh->bnih', attn, v)
        o = o.transpose(0, 2, 1, 3).reshape(b, l, d)
        return o @ Wo.T + bo

    def _L0_ffn_ref(x, wg, bg, Wgate, Wup, Wdown):
        import jax, jax.numpy as jnp
        import numpy as np
        NUM_EXPERTS = 8
        TOP_K = 2
        DIM = 128
        HIDDEN = 512
        B, S = (4, 256)
        b, s, d = x.shape
        xf = x.reshape(-1, d)
        T = xf.shape[0]
        logits = xf @ wg.T + bg
        vals, idx = jax.lax.top_k(logits, TOP_K)
        masked = jnp.full_like(logits, -jnp.inf)
        rows = jnp.arange(T)[:, None]
        masked = masked.at[rows, idx].set(vals)
        weights = jax.nn.softmax(masked, axis=-1)
        out = jnp.zeros_like(xf)
        for e in range(NUM_EXPERTS):
            g = xf @ Wgate[e].T
            u = xf @ Wup[e].T
            h = g * jax.nn.sigmoid(g) * u
            out = out + h @ Wdown[e].T * weights[:, e:e + 1]
        return out.reshape(b, s, d)
    x = L0_attn_a_x
    x = x + _L0_attn_a_ref(_layernorm(x, axis=-1), L0_attn_a_Wq, L0_attn_a_Wk, L0_attn_a_Wv, L0_attn_a_Wff, L0_attn_a_bff)
    x = x + _L0_ffn_ref(_layernorm(x, axis=-1), L0_ffn_wg, L0_ffn_bg, L0_ffn_Wgate, L0_ffn_Wup, L0_ffn_Wdown)
    x = x + _L0_attn_b_ref(_layernorm(x, axis=-1), L0_attn_b_Wq, L0_attn_b_bq, L0_attn_b_Wk, L0_attn_b_bk, L0_attn_b_Wv, L0_attn_b_bv, L0_attn_b_Wo, L0_attn_b_bo, L0_attn_b_scale)
    x = x + _L0_ffn_ref(_layernorm(x, axis=-1), L0_ffn_wg, L0_ffn_bg, L0_ffn_Wgate, L0_ffn_Wup, L0_ffn_Wdown)
    return x

_drawn_inputs = setup_inputs


def setup_inputs(seed=0):
    import zlib

    import numpy as np

    out = dict(_drawn_inputs(seed))
    spreads = {'L0_ffn_bg': (0.0, 0.8)}
    factors = {'L0_attn_a_bff': 4.786,
     'L0_attn_b_Wq': 8.0,
     'L0_attn_b_bq': 8.0,
     'L0_attn_b_Wk': 8.0,
     'L0_attn_b_bk': 8.0,
     'L0_attn_b_Wv': 6.736,
     'L0_attn_b_bv': 8.0,
     'L0_attn_b_Wo': 5.982,
     'L0_attn_b_bo': 2.706,
     'L0_ffn_wg': 4.012,
     'L0_ffn_Wgate': 3.407,
     'L0_ffn_Wup': 3.401,
     'L0_ffn_Wdown': 3.397}
    for name, (base, spread) in spreads.items():
        noise = np.random.default_rng([zlib.crc32(name.encode()), seed]).standard_normal(out[name].shape)
        drawn = base * np.exp(spread * noise) if base else spread * noise
        out[name] = jnp.asarray(drawn.astype(out[name].dtype))
    for name, factor in factors.items():
        out[name] = (out[name] * factor).astype(out[name].dtype)
    return out
```

```python
from contextlib import ExitStack

import numpy as np
import concourse.bass as bass
from concourse import mybir

F32 = mybir.dt.float32
F32R = mybir.dt.float32r
BF16 = mybir.dt.bfloat16
I32 = mybir.dt.int32
ACT = mybir.ActivationFunctionType
ALU = mybir.AluOpType
AX = mybir.AxisListType

B, S, D = 16, 256, 128
HEADS = 16
DH = D // HEADS
TOKENS = B * S
P = 128
TILES = TOKENS // P
QUAD = 4
GROUPS = HEADS // QUAD
STEPS = B * GROUPS
ROUNDS = TILES // QUAD
ROW = 32
SHIFT_ROW = 3 * DH
EXPERTS = 8
HIDDEN = 512
CHUNKS = HIDDEN // P
SLOT_TILES = 2 * TILES + EXPERTS
EPS = 1e-5
MASKED = -100000.0
THETA = 10000.0
Q_SCALE_A = float(1.0 / np.sqrt(np.float32(D)))
BIG = 3.0e38

C_IDENT = 0
C_TRI = C_IDENT + P
C_COS = C_TRI + P
C_SIN = C_COS + S
C_KBIAS = C_SIN + S
C_RANK = C_KBIAS + 1
C_START = C_RANK + EXPERTS
C_KEEP = C_START + SLOT_TILES
C_MASKS = 0
C_PERM = 2 * 2 * S
N_PERM = 4 * GROUPS * P
C_STAGED = C_PERM + N_PERM


def at_least(engine, semaphore, value):
    if not (isinstance(value, int) and value <= 0):
        engine.wait_ge(semaphore, value)


def pipelined(engine, body, first, n, steps, unroll):
    assert first % unroll == 0 and (n - first) % unroll == 0
    for t in range(first):
        body(t, t % unroll)
    with engine.Fori(0, (n - first) // unroll) as turn:
        for u in range(unroll):
            body(turn * unroll + (first + u), u)
    for t in range(n, steps):
        body(t, t % unroll)


class Hybrid:

    def __init__(self, nc, ctx, dram):
        self.nc, self.ctx, self.dram = nc, ctx, dram
        sb = self.sb
        self.X = sb("X", [P, TILES, D])
        self.work = sb("work", [P, TILES, D])
        self.q_hi = sb("q_hi", [P, TOKENS], F32R)
        self.q_lo = sb("q_lo", [P, TOKENS], F32R)
        self.k_hi = sb("k_hi", [P, TOKENS], F32R)
        self.k_lo = sb("k_lo", [P, TOKENS], F32R)
        self.w_gate = sb("w_gate", [P, EXPERTS * HIDDEN])
        self.w_up = sb("w_up", [P, EXPERTS * HIDDEN])
        self.w_down = sb("w_down", [P, EXPERTS * CHUNKS * D])
        self.scratch = sb("scratch", [P, 5632])
        self.consts = sb("consts", [P, C_KEEP])
        self.perm = sb("perm", [P, N_PERM], F32R)
        self.masks = sb("masks", [P, 2, 2 * S], BF16)
        self.ident_b = sb("ident_b", [P, P], BF16)
        self.ones = sb("ones", [P, P])
        self.eps4 = sb("eps4", [P, 1])
        self.stack = [sb(f"stack{i}", [P, 2 * S], F32R) for i in range(2)]
        self.q_shifted = [sb(f"q_shifted{i}", [P, S], F32R) for i in range(2)]
        self.row_max = [sb(f"row_max{i}", [P, 2, QUAD, ROW]) for i in range(2)]
        self.v_ones = [sb(f"v_ones{g}", [P, 2, QUAD, ROW]) for g in range(GROUPS)]
        self.out_t = [sb(f"out_t{i}", [P, S]) for i in range(2)]
        self.rec_den = sb("rec_den", [P, 2, QUAD])
        self.logits = sb("logits", [P, TILES, EXPERTS])
        self.slot = [sb(f"slot{i}", [P, TILES], I32) for i in range(2)]
        self.gate = [sb(f"gate{i}", [P, TILES]) for i in range(2)]
        self.tile_expert = sb("tile_expert", [P, SLOT_TILES], I32)
        self.stats = sb("stats", [P, QUAD, 6])
        self.mean_var = [sb(f"mean_var{i}", [P, QUAD, 2]) for i in range(2)]
        self.root = [sb(f"root{i}", [P, QUAD]) for i in range(2)]
        self.carrier = sb("carrier", [P, 1])
        self.inv = sb("inv", [P, QUAD])
        self.inv2 = sb("inv2", [P, QUAD])
        self.rstd = [sb(f"rstd{i}", [P, QUAD]) for i in range(2)]
        self.w_att = {n: sb(f"w_{n}", [P, D]) for n in
                      ("a_q", "a_k", "a_v", "a_o", "b_q", "b_k", "b_qs", "b_ks", "b_v", "b_o")}
        self.bias = {n: sb(f"bias_{n}", [P, 1]) for n in ("q", "k", "qs", "ks", "scale")}
        self.rows = {n: sb(f"rows_{n}", [P, D]) for n in ("a_o", "b_v", "b_o")}
        self.w_route = sb("w_route", [P, EXPERTS])
        self.b_route = sb("b_route", [P, EXPERTS])
        self.PS = ctx.enter_context(nc.psum_tensor("PS", [P, 8, 512], F32))
        self.x_slots = nc.dram_tensor("x_slots", (SLOT_TILES * P, D), F32, kind="Internal").ap()
        self.y_slots = nc.dram_tensor("y_slots", (SLOT_TILES * P, D), F32, kind="Internal").ap()
        self.ident = self.consts[:, C_IDENT:C_IDENT + P]
        self.tri = self.consts[:, C_TRI:C_TRI + P]
        self.experts_loaded = self.sem("experts_loaded")
        self.slots_zeroed = self.sem("slots_zeroed")

    def sb(self, name, shape, dt=F32):
        return self.ctx.enter_context(self.nc.sbuf_tensor(name, shape, dt))

    def sem(self, name):
        return self.ctx.enter_context(self.nc.semaphore(name))

    def setup(self):
        nc, d = self.nc, self.dram
        loaded, staged, cleared, masked = (self.sem(n) for n in
                                           ("const_loaded", "staged", "cleared", "mask_made"))
        zero = self.q_shifted
        del zero
        table = self.scratch[:, 0:C_STAGED]
        blank = self.scratch[:, C_STAGED:C_STAGED + 2 * P * 5]
        n_small = 0
        with nc.Block() as block:
            @block.sync
            def _(sp):
                sp.dma_start(table, d["staged"]).then_inc(staged, 16)
                sp.dma_start(self.consts[:, :], d["consts"]).then_inc(loaded, 16)
                x = d["x"].rearrange("(t p) d -> p t d", p=P)
                for c in range(4):
                    t = slice(c * TILES // 4, (c + 1) * TILES // 4)
                    sp.dma_start(self.X[:, t, :], x[:, t, :]).then_inc(loaded, 16)
                for n, w in self.w_att.items():
                    sp.dma_start(w[:, :], d[f"w_{n}"]).then_inc(loaded, 16)
                sp.dma_start(self.w_route[:, :], d["w_route"]).then_inc(loaded, 16)
                sp.dma_start(self.w_gate[:, :], d["w_gate"]).then_inc(self.experts_loaded, 16)
                sp.dma_start(self.w_up[:, :], d["w_up"]).then_inc(self.experts_loaded, 16)
                sp.dma_start(self.w_down[:, :], d["w_down"]).then_inc(self.experts_loaded, 16)
                sp.wait_ge(cleared, 1)
                flat = self.x_slots.rearrange("(p r) d -> p (r d)", p=P)
                for c in range(SLOT_TILES // 8):
                    sp.dma_start(flat[:, c * 8 * D:(c + 1) * 8 * D],
                                 blank[:, 0:8 * D]).then_inc(self.slots_zeroed, 16)
                sp.wait_ge(loaded, 16 * (6 + len(self.w_att)))
                sp.wait_ge(self.slots_zeroed, 16 * (SLOT_TILES // 8))

            @block.scalar
            def _(act):
                small = self.sem("small_loaded")
                n = 0
                for name, b in self.bias.items():
                    src = d[f"bias_{name}"]
                    if name == "scale":
                        src = src.rearrange("(o n) -> o n", o=1).to_broadcast((P, 1))
                    else:
                        src = src.rearrange("(p o) -> p o", o=1)
                    act.dma_start(b[:, :], src).then_inc(small, 16)
                    n += 16
                for name, r in self.rows.items():
                    act.dma_start(r[:, :], d[f"rows_{name}"].rearrange("(o n) -> o n", o=1)
                                  .to_broadcast((P, D))).then_inc(small, 16)
                    n += 16
                act.dma_start(self.b_route[:, :], d["b_route"].rearrange("(o n) -> o n", o=1)
                              .to_broadcast((P, EXPERTS))).then_inc(small, 16)
                act.wait_ge(small, n + 16)

            @block.gpsimd
            def _(pool):
                pool.memset(blank, 0.0).then_inc(cleared, 1)
                for i in range(2):
                    pool.memset(self.row_max[i][:, :, :, :], 0.0)
                for g in range(GROUPS):
                    pool.memset(self.v_ones[g][:, :, :, :], 0.0).then_inc(cleared, 1)
                    pool.wait_ge(cleared, g + 2)
                    pool.memset(self.v_ones[g][:, :, :, DH:DH + 1], 1.0)
                pool.memset(self.ones[:, :], 1.0)
                pool.memset(self.eps4[:, :], EPS / 4)

            @block.vector
            def _(dve):
                dve.wait_ge(staged, 16)
                dve.tensor_copy(self.perm[:, :], table[:, C_PERM:C_PERM + N_PERM])
                dve.tensor_copy(self.masks[:, :, :].rearrange("p a n -> p (a n)"),
                                table[:, C_MASKS:C_MASKS + 4 * S])
                dve.wait_ge(loaded, 16 * (6 + len(self.w_att)))
                dve.tensor_copy(self.ident_b[:, :], self.ident).then_inc(masked, 1)

    def norm_sems(self, tag):
        return {n: self.sem(f"{tag}_{n}") for n in
                ("stats_done", "var_done", "root_done", "newton_done", "xn_done")}

    def carry_wait(self, dve):
        dve.memset(self.carrier[:, :], 0.0)

    def norm_stats(self, dve, i, u, s):
        self.carry_wait(dve)
        for j in range(QUAD):
            dve.bn_stats(self.stats[:, j, :], self.X[:, QUAD * i + j, :]).then_inc(s["stats_done"], 1)
        dve.wait_ge(s["stats_done"], QUAD * i + QUAD)
        self.carry_wait(dve)
        for j in range(QUAD):
            dve.bn_aggr(self.mean_var[u][:, j, :], self.stats[:, j, :]).then_inc(s["var_done"], 1)

    def norm_root(self, act, i, u, s):
        act.wait_ge(s["var_done"], QUAD * i + QUAD)
        act.activation(self.root[u][:, :], self.mean_var[u][:, :, 1], ACT.Sqrt,
                       bias=self.eps4[:, :], scale=0.25).then_inc(s["root_done"], 1)

    def norm_rows(self, dve, i, u, s, xn):
        dve.wait_ge(s["root_done"], i + 1)
        step = s["newton_done"]
        dve.reciprocal(self.inv[:, :], self.root[u][:, :]).then_inc(step, 1)
        dve.tensor_scalar(self.inv2[:, :], self.mean_var[u][:, :, 1], EPS, 0.25, ALU.add,
                          ALU.mult).then_inc(step, 1)
        dve.wait_ge(step, 5 * i + 2)
        dve.tensor_tensor(self.inv2[:, :], self.inv2[:, :], self.inv[:, :], ALU.mult).then_inc(step, 1)
        dve.wait_ge(step, 5 * i + 3)
        dve.tensor_tensor(self.inv[:, :], self.inv2[:, :], self.root[u][:, :], ALU.add).then_inc(step, 1)
        dve.wait_ge(step, 5 * i + 4)
        dve.reciprocal(self.rstd[u][:, :], self.inv[:, :]).then_inc(step, 1)
        dve.wait_ge(step, 5 * i + 5)
        for j in range(QUAD):
            dve.tensor_scalar(xn[:, j, :], self.X[:, QUAD * i + j, :], self.mean_var[u][:, j, 0:1],
                              self.rstd[u][:, j:j + 1], ALU.subtract, ALU.mult).then_inc(s["xn_done"], 1)

    def ring(self, at, n, *dims):
        out = []
        for i in range(2):
            v = self.scratch[:, at + i * n:at + (i + 1) * n]
            if dims:
                v = v.rearrange("p (t d) -> p t d", t=dims[0])
            out.append(v)
        return out

    def project(self, tag, rotary):
        nc, PS = self.nc, self.PS
        s = self.norm_sems(tag)
        xT_done, xT_ready, proj_done, v_done, hi_ready, rot_done, qk_used, v_used = (
            self.sem(f"{tag}_{n}") for n in ("xT_done", "xT_ready", "proj_done", "v_done", "hi_ready",
                                             "rot_done", "qk_used", "v_used"))
        xn = self.ring(0, 512, QUAD)
        xT = self.ring(1024, 512)
        turned = [self.scratch[:, 2048 + 512 * i:2560 + 512 * i] for i in range(2)]
        part = [self.scratch[:, 3072 + 512 * i:3584 + 512 * i] for i in range(4)]
        kinds = ("q", "k", "qs", "ks") if rotary else ("q", "k")
        L = "b" if rotary else "a"
        T_BANK, V_BANK = 0, 7
        bank = {"q": 1, "k": 2, "qs": 3, "ks": 4}
        hi = {"q": self.q_hi, "k": self.k_hi}
        lo = {"q": self.q_lo, "k": self.k_lo}
        cols = lambda i: bass.ds(i * 512, 512)

        with nc.Block() as block:
            @block.vector
            def _(dve):
                def rotate(i):
                    for n, kind in enumerate(("q", "k")):
                        for m, (src, trig) in enumerate(((kind, C_COS), (kind + "s", C_SIN))):
                            dve.wait_ge(proj_done, len(kinds) * i + kinds.index(src) + 1)
                            dve.scalar_tensor_tensor(
                                out=part[2 * n + m].rearrange("p (b s) -> p b s", b=2),
                                in0=PS[:, bank[src], :].rearrange("p (b s) -> p b s", b=2),
                                scalar=self.bias[src][:, 0:1],
                                in1=self.consts[:, trig:trig + S].unsqueeze(1).to_broadcast((P, 2, S)),
                                op0=ALU.add, op1=ALU.mult).then_inc(rot_done, 1)
                        dve.wait_ge(rot_done, 6 * i + 3 * n + 2)
                        dve.tensor_tensor(turned[n], part[2 * n], part[2 * n + 1], ALU.add)\
                           .then_inc(rot_done, 1)

                def low_parts(i):
                    for n, kind in enumerate(("q", "k")):
                        dve.wait_ge(hi_ready, 2 * i + n + 1)
                        value = turned[n] if rotary else PS[:, bank[kind], :]
                        scale = (self.bias["scale"][:, 0:1] if rotary else Q_SCALE_A) if kind == "q" else 1.0
                        dve.scalar_tensor_tensor(out=lo[kind][:, cols(i)], in0=value, scalar=scale,
                                                 in1=hi[kind][:, cols(i)].bitcast(F32), op0=ALU.mult,
                                                 op1=ALU.subtract).then_inc(qk_used, 1)

                def body(t, u):
                    if not (isinstance(t, int) and t >= ROUNDS):
                        self.norm_stats(dve, t, u, s)
                    if not (isinstance(t, int) and t < 1):
                        i = t - 1
                        if rotary:
                            rotate(i)
                        low_parts(i)
                        if rotary:
                            dve.wait_ge(v_done, i + 1)
                            dve.tensor_tensor(self.work[:, bass.ds(QUAD * i, QUAD), :],
                                              PS[:, V_BANK, :].rearrange("p (t d) -> p t d", t=QUAD),
                                              self.rows["b_v"][:, :].unsqueeze(1).to_broadcast((P, QUAD, D)),
                                              ALU.add).then_inc(v_used, 1)
                    if not (isinstance(t, int) and t >= ROUNDS):
                        self.norm_rows(dve, t, u, s, xn[u])

                pipelined(dve, body, 2, ROUNDS, ROUNDS + 1, 2)

            @block.tensor
            def _(pe):
                def body(i, u):
                    pe.wait_ge(s["xn_done"], QUAD * i + QUAD)
                    at_least(pe, xT_ready, i)
                    for j in range(QUAD):
                        mm = pe.transpose(PS[:, T_BANK, j * P:(j + 1) * P], xn[u][:, j, :], self.ident)
                    mm.then_inc(xT_done, 1)
                    pe.wait_ge(xT_ready, i + 1)
                    at_least(pe, qk_used, 2 * i)
                    for kind in kinds:
                        pe.matmul(PS[:, bank[kind], :], self.w_att[f"{L}_{kind}"][:, :], xT[u],
                                  start=True, stop=True).then_inc(proj_done, 1)
                    at_least(pe, v_used, i)
                    for j in range(QUAD):
                        mm = pe.matmul(PS[:, V_BANK, j * D:(j + 1) * D], xT[u][:, j * P:(j + 1) * P],
                                       self.w_att[f"{L}_v"][:, :], start=True, stop=True)
                    mm.then_inc(v_done, 1)

                pipelined(pe, body, 2, ROUNDS, ROUNDS, 2)

            @block.scalar
            def _(act):
                def body(t, u):
                    if not (isinstance(t, int) and t >= ROUNDS):
                        self.norm_root(act, t, u, s)
                    if not (isinstance(t, int) and t < 1):
                        i = t - 1
                        for n, kind in enumerate(("q", "k")):
                            if rotary:
                                act.wait_ge(rot_done, 6 * i + 3 * n + 3)
                            else:
                                act.wait_ge(proj_done, 2 * i + n + 1)
                            value = turned[n] if rotary else PS[:, bank[kind], :]
                            scale = (self.bias["scale"][:, 0:1] if rotary else Q_SCALE_A) if kind == "q" else 1.0
                            act.activation(hi[kind][:, cols(i)], value, ACT.Copy, scale=scale)\
                               .then_inc(hi_ready, 1)
                        if not rotary:
                            act.wait_ge(v_done, i + 1)
                            act.activation(self.work[:, bass.ds(QUAD * i, QUAD), :],
                                           PS[:, V_BANK, :].rearrange("p (t d) -> p t d", t=QUAD),
                                           ACT.Copy).then_inc(v_used, 1)
                    if not (isinstance(t, int) and t >= ROUNDS):
                        act.wait_ge(xT_done, t + 1)
                        act.activation(xT[u], PS[:, T_BANK, :], ACT.Copy).then_inc(xT_ready, 1)

                pipelined(act, body, 2, ROUNDS, ROUNDS + 1, 2)

    def attend(self, tag, causal):
        nc, PS = self.nc, self.PS
        (stack_done, stack_ready, score_done, max_ready, shift_done, q_ready, scoreT_done, probs_ready,
         pv_done, outT_ready, out_done, rec_ready, out_used, v_ready) = (
            self.sem(f"{tag}_{n}") for n in
            ("stack_done", "stack_ready", "score_done", "max_ready", "shift_done", "q_ready",
             "scoreT_done", "probs_ready", "pv_done", "outT_ready", "out_done", "rec_ready",
             "out_used", "v_ready"))
        probs = [self.scratch[:, 2048 * i:2048 * (i + 1)].rearrange("p (j n) -> p j n", j=QUAD)
                 for i in range(2)]
        KEYS_BANK, SCORE_BANK, PV_BANK, STACK_BANK = 0, 4, 6, 7

        def stages(t):
            if isinstance(t, int):
                return t < STEPS, 1 <= t <= STEPS, t >= 2
            return True, True, True

        with nc.Block() as block:
            @block.tensor
            def _(pe):
                def stack_parts(t, g):
                    at_least(pe, q_ready, t)
                    tokens = bass.ds((t - g) * (S // GROUPS), S)
                    for n, parts in enumerate(((self.q_hi, self.q_lo), (self.k_hi, self.k_lo))):
                        for m, part in enumerate(parts):
                            c = ((2 * n + m) * GROUPS + g) * P
                            mm = pe.matmul(PS[:, STACK_BANK, n * S:(n + 1) * S], self.perm[:, c:c + P],
                                           part[:, tokens], start=(m == 0), stop=(m == 1))
                    mm.then_inc(stack_done, 1)

                def scores(t, u, j):
                    at_least(pe, max_ready, QUAD * t + j - 1)
                    out = PS[:, SCORE_BANK + j % 2, :]
                    r = slice(ROW * j, ROW * j + ROW)
                    if causal:
                        pe.matmul(out, self.ident_b[:, :], self.masks[:, 0, :], start=True, stop=False,
                                  skip_group_check=True)
                    for q in range(2):
                        mm = pe.matmul(out[:, q * S:(q + 1) * S], self.stack[u][r, q * P:(q + 1) * P],
                                       self.stack[u][r, S:2 * S], start=not causal, stop=True,
                                       skip_group_check=True)
                    mm.then_inc(score_done, 1)

                def scores_t(s, u, half):
                    at_least(pe, probs_ready, 2 * s + half - 1)
                    for j in (2 * half, 2 * half + 1):
                        out = PS[:, KEYS_BANK + j, :]
                        r = slice(ROW * j, ROW * j + ROW)
                        if causal:
                            pe.matmul(out, self.ident_b[:, :], self.masks[:, 1, :], start=True,
                                      stop=False, skip_group_check=True)
                        for k in range(2):
                            mm = pe.matmul(out[:, k * S:(k + 1) * S],
                                           self.stack[u][r, S + k * P:S + (k + 1) * P],
                                           self.q_shifted[u][r, :], start=not causal, stop=True,
                                           skip_group_check=True)
                    mm.then_inc(scoreT_done, 1)

                def body(t, g):
                    one, two, three = stages(t)
                    u = g % 2
                    if one:
                        stack_parts(t, g)
                    if two:
                        pe.wait_ge(q_ready, t)
                        scores_t(t - 1, 1 - u, 0)
                    if one:
                        pe.wait_ge(stack_ready, 2 * t + 2)
                        scores(t, u, 0)
                        scores(t, u, 1)
                    if two:
                        scores_t(t - 1, 1 - u, 1)
                    if one:
                        scores(t, u, 2)
                        scores(t, u, 3)
                    if three:
                        s = t - 2
                        pe.wait_ge(probs_ready, 2 * s + 2)
                        pe.wait_ge(v_ready, s + 1)
                        at_least(pe, out_used, s)
                        for k in range(2):
                            for j in range(QUAD):
                                mm = pe.matmul(PS[ROW * j:ROW * j + ROW, PV_BANK, 0:S],
                                               self.v_ones[(g - 2) % GROUPS][:, k, j, :],
                                               probs[u][:, j, k * S:(k + 1) * S],
                                               start=(k == 0), stop=(k == 1), skip_group_check=True)
                        mm.then_inc(pv_done, 1)
                    if one:
                        pe.wait_ge(max_ready, QUAD * t + QUAD)
                        for q in range(2):
                            mm = pe.transpose(PS[:, STACK_BANK, q * P:(q + 1) * P],
                                              self.row_max[u][:, q, :, :].rearrange("p j r -> p (j r)"),
                                              self.ident)
                        mm.then_inc(shift_done, 1)
                    if three:
                        pe.wait_ge(outT_ready, s + 1)
                        for q in range(2):
                            mm = pe.transpose(PS[:, PV_BANK, S + q * P:S + (q + 1) * P],
                                              self.out_t[u][:, q * P:(q + 1) * P], self.ident)
                        mm.then_inc(out_done, 1)

                pipelined(pe, body, 4, STEPS, STEPS + 2, 4)

            @block.scalar
            def _(act):
                def body(t, g):
                    one, two, three = stages(t)
                    u = g % 2
                    if one:
                        act.wait_ge(stack_done, t + 1)
                        act.activation(self.stack[u][:, 0:S], PS[:, STACK_BANK, 0:S], ACT.Copy)\
                           .then_inc(stack_ready, 1)
                        act.activation(self.stack[u][:, S:2 * S], PS[:, STACK_BANK, S:2 * S], ACT.Identity,
                                       bias=self.consts[:, C_KBIAS:C_KBIAS + 1]).then_inc(stack_ready, 1)
                    if two:
                        s = t - 1
                        for half in range(2):
                            act.wait_ge(scoreT_done, 2 * s + half + 1)
                            at_least(act, pv_done, s - 1)
                            act.activation(probs[1 - u][:, 2 * half:2 * half + 2, :],
                                           PS[:, KEYS_BANK + 2 * half:KEYS_BANK + 2 * half + 2, :],
                                           ACT.Exp).then_inc(probs_ready, 1)
                    if three:
                        s = t - 2
                        act.wait_ge(pv_done, s + 1)
                        act.activation(self.out_t[u][:, :], PS[:, PV_BANK, 0:S], ACT.Copy)\
                           .then_inc(outT_ready, 1)

                pipelined(act, body, 4, STEPS, STEPS + 2, 4)

            @block.vector
            def _(dve):
                def body(t, g):
                    one, two, three = stages(t)
                    u = g % 2
                    if one:
                        for j in range(QUAD):
                            dve.wait_ge(score_done, QUAD * t + j + 1)
                            dve.tensor_reduce(self.row_max[u][:, :, j, SHIFT_ROW:SHIFT_ROW + 1],
                                              PS[:, SCORE_BANK + j % 2, :].rearrange("p (q k) -> p q k", q=2),
                                              AX.X, ALU.max).then_inc(max_ready, 1)
                        dve.wait_ge(shift_done, t + 1)
                        dve.tensor_tensor(self.q_shifted[u][:, :], self.stack[u][:, 0:S].bitcast(F32),
                                          PS[:, STACK_BANK, 0:S], ALU.subtract).then_inc(q_ready, 1)
                    if three:
                        s = t - 2
                        dve.wait_ge(out_done, s + 1)
                        rows = PS[:, PV_BANK, S:2 * S].rearrange("p (q j r) -> p q j r", q=2, j=QUAD)
                        dve.reciprocal(self.rec_den[:, :, :], rows[:, :, :, DH]).then_inc(rec_ready, 1)
                        dve.wait_ge(rec_ready, s + 1)
                        gg = (g - 2) % GROUPS
                        tiles = bass.ds((s - gg) * 2 // GROUPS if isinstance(s, int)
                                        else (t - (gg + 2)) // 2, 2)
                        out = self.work[:, tiles, ROW * gg:ROW * gg + ROW]\
                            .rearrange("p q (j d) -> p q j d", j=QUAD)
                        dve.tensor_tensor(out, rows[:, :, :, 0:DH],
                                          self.rec_den[:, :, :].unsqueeze(3).to_broadcast((P, 2, QUAD, DH)),
                                          ALU.mult).then_inc(out_used, 1)

                pipelined(dve, body, 4, STEPS, STEPS + 2, 4)

            @block.gpsimd
            def _(pool):
                def body(s, g):
                    at_least(pool, pv_done, s - 3)
                    tiles = bass.ds((s - g) // 2, 2)
                    pool.tensor_copy(self.v_ones[g][:, :, :, 0:DH],
                                     self.work[:, tiles, ROW * g:ROW * g + ROW]
                                     .rearrange("p q (j d) -> p q j d", j=QUAD)).then_inc(v_ready, 1)

                pipelined(pool, body, 4, STEPS, STEPS, 4)

    def finish(self, tag):
        nc, PS = self.nc, self.PS
        L = tag[0]
        s = self.norm_sems(tag + "_f")
        (att_copied, aT_done, aT_ready, o_done, o_used, x_ready, xT_done, xT_ready, lg_done, lg_used,
         kept0, kept1) = (
            self.sem(f"{tag}_f_{n}") for n in
            ("att_copied", "aT_done", "aT_ready", "o_done", "o_used", "x_ready", "xT_done", "xT_ready",
             "lg_done", "lg_used", "kept0", "kept1"))
        kept = [kept0, kept1]
        att = self.ring(0, 512, QUAD)
        aT = self.ring(1024, 512)
        xn = self.ring(2048, 512, QUAD)
        xT = self.ring(3072, 512)
        AT_BANK, O_BANK, XT_BANK, LG_BANK = 0, 1, 3, 4

        def stages(t):
            if isinstance(t, int):
                return t < ROUNDS, t >= 1
            return True, True

        with nc.Block() as block:
            @block.gpsimd
            def _(pool):
                def body(i, u):
                    at_least(pool, aT_done, i - 1)
                    pool.tensor_copy(att[u], self.work[:, bass.ds(QUAD * i, QUAD), :])\
                        .then_inc(att_copied, 1)

                pipelined(pool, body, 2, ROUNDS, ROUNDS, 2)

            @block.tensor
            def _(pe):
                def body(t, u):
                    one, two = stages(t)
                    if one:
                        pe.wait_ge(att_copied, t + 1)
                        at_least(pe, aT_ready, t)
                        for j in range(QUAD):
                            mm = pe.transpose(PS[:, AT_BANK, j * P:(j + 1) * P], att[u][:, j, :], self.ident)
                        mm.then_inc(aT_done, 1)
                        pe.wait_ge(aT_ready, t + 1)
                        at_least(pe, o_used, t - 1)
                        for j in range(QUAD):
                            mm = pe.matmul(PS[:, O_BANK + u, j * D:(j + 1) * D], aT[u][:, j * P:(j + 1) * P],
                                           self.w_att[f"{L}_o"][:, :], start=True, stop=True)
                        mm.then_inc(o_done, 1)
                    if two:
                        i = t - 1
                        pe.wait_ge(s["xn_done"], QUAD * i + QUAD)
                        at_least(pe, xT_ready, i)
                        for j in range(QUAD):
                            mm = pe.transpose(PS[:, XT_BANK, j * P:(j + 1) * P], xn[1 - u][:, j, :], self.ident)
                        mm.then_inc(xT_done, 1)
                        pe.wait_ge(xT_ready, i + 1)
                        at_least(pe, lg_used, i)
                        for j in range(QUAD):
                            mm = pe.matmul(PS[:, LG_BANK, j * EXPERTS:(j + 1) * EXPERTS],
                                           xT[1 - u][:, j * P:(j + 1) * P], self.w_route[:, :],
                                           start=True, stop=True)
                        mm.then_inc(lg_done, 1)

                pipelined(pe, body, 2, ROUNDS, ROUNDS + 1, 2)

            @block.scalar
            def _(act):
                def body(t, u):
                    one, two = stages(t)
                    if one:
                        act.wait_ge(aT_done, t + 1)
                        act.activation(aT[u], PS[:, AT_BANK, :], ACT.Copy).then_inc(aT_ready, 1)
                    if two:
                        i = t - 1
                        act.wait_ge(xT_done, i + 1)
                        act.activation(xT[1 - u], PS[:, XT_BANK, :], ACT.Copy).then_inc(xT_ready, 1)
                    if one:
                        self.norm_root(act, t, u, s)

                pipelined(act, body, 2, ROUNDS, ROUNDS + 1, 2)

            @block.vector
            def _(dve):
                def body(t, u):
                    one, two = stages(t)
                    if one:
                        X4 = self.X[:, bass.ds(QUAD * t, QUAD), :]
                        dve.wait_ge(o_done, t + 1)
                        dve.tensor_tensor(X4, PS[:, O_BANK + u, :].rearrange("p (t d) -> p t d", t=QUAD),
                                          X4, ALU.add).then_inc(o_used, 1)
                        dve.wait_ge(o_used, t + 1)
                        dve.tensor_tensor(X4, X4, self.rows[f"{L}_o"][:, :].unsqueeze(1)
                                          .to_broadcast((P, QUAD, D)), ALU.add).then_inc(x_ready, 1)
                        dve.wait_ge(x_ready, t + 1)
                        self.norm_stats(dve, t, u, s)
                    if two:
                        i = t - 1
                        dve.wait_ge(lg_done, i + 1)
                        dve.tensor_tensor(self.logits[:, bass.ds(QUAD * i, QUAD), :],
                                          PS[:, LG_BANK, 0:QUAD * EXPERTS].rearrange("p (t e) -> p t e", t=QUAD),
                                          self.b_route[:, :].unsqueeze(1).to_broadcast((P, QUAD, EXPERTS)),
                                          ALU.add).then_inc(lg_used, 1)
                    if one:
                        at_least(dve, kept[u], 8 * (t - u) if not isinstance(t, int) else 16 * (t // 2))
                        self.norm_rows(dve, t, u, s, xn[u])

                pipelined(dve, body, 2, ROUNDS, ROUNDS + 1, 2)

            @block.sync
            def _(sp):
                def body(i, u):
                    sp.wait_ge(s["xn_done"], QUAD * i + QUAD)
                    sp.dma_start(self.work[:, bass.ds(QUAD * i, QUAD), :], xn[u]).then_inc(kept[u], 16)

                pipelined(sp, body, 2, ROUNDS, ROUNDS, 2)
                for k in kept:
                    sp.wait_ge(k, 16 * (ROUNDS // 2))

    def route(self, tag):
        nc, PS = self.nc, self.PS
        done, counted, exp_in, exp_out, scattered = (
            self.sem(f"{tag}_r_{n}") for n in ("done", "counted", "exp_in", "exp_out", "scattered"))
        N = TILES * EXPERTS
        big = [self.scratch[:, N * i:N * (i + 1)].rearrange("p (t e) -> p t e", e=EXPERTS)
               for i in range(10)]
        mask1, mask2, picked, tmp, tmp2, total, run0, run1, place, _unused = big
        at = 10 * N
        vec = [self.scratch[:, at + TILES * i:at + TILES * (i + 1)] for i in range(8)]
        m1, m2, mx, diff, ratio, one_plus, pos, _v = vec
        at += 8 * TILES
        eight = [self.scratch[:, at + EXPERTS * i:at + EXPERTS * (i + 1)] for i in range(8)]
        e_cnt, e_a, e_b, e_c, e_base, e_end, e_x, e_y = eight
        at += 8 * EXPERTS
        cmp = self.scratch[:, at:at + SLOT_TILES * EXPERTS].rearrange("p (i e) -> p i e", e=EXPERTS)
        at += SLOT_TILES * EXPERTS
        cnt = self.scratch[:, at:at + SLOT_TILES]
        ints = self.tile_expert[:, 0:EXPERTS]
        wide = lambda v: v.unsqueeze(2).to_broadcast((P, TILES, EXPERTS))
        per_tile = lambda v: v.unsqueeze(1).to_broadcast((P, TILES, EXPERTS))
        rank = self.consts[:, C_RANK:C_RANK + EXPERTS]
        starts = self.consts[:, C_START:C_START + SLOT_TILES]

        with nc.Block() as block:
            @block.vector
            def _(dve):
                count = [0]

                def then(ins):
                    count[0] += 1
                    ins.then_inc(done, 1)
                    dve.wait_ge(done, count[0])

                def best(values, best_value, mask):
                    then(dve.tensor_reduce(best_value, values, AX.X, ALU.max))
                    then(dve.tensor_tensor(tmp, values, wide(best_value), ALU.is_equal))
                    then(dve.tensor_tensor(tmp2, tmp, per_tile(rank), ALU.mult))
                    then(dve.tensor_reduce(mx, tmp2, AX.X, ALU.max))
                    then(dve.tensor_tensor(mask, tmp2, wide(mx), ALU.is_equal))

                best(self.logits[:, :, :], m1, mask1)
                then(dve.scalar_tensor_tensor(out=place, in0=mask1, scalar=-BIG, in1=self.logits[:, :, :],
                                              op0=ALU.mult, op1=ALU.add))
                best(place, m2, mask2)
                then(dve.tensor_tensor(picked, mask1, mask2, ALU.add))
                dve.tensor_tensor(diff, m2, m1, ALU.subtract).then_inc(exp_in, 1)
                dve.wait_ge(counted, 2)
                then(dve.tensor_copy(total, PS[:, 1, 0:N].rearrange("p (t e) -> p t e", e=EXPERTS)))
                src, dst = total, run0
                k = 1
                while k < TILES:
                    then(dve.tensor_copy(dst[:, 0:k, :], src[:, 0:k, :]))
                    then(dve.tensor_tensor(dst[:, k:TILES, :], src[:, k:TILES, :], src[:, 0:TILES - k, :],
                                           ALU.add))
                    src, dst = dst, (run1 if dst is run0 else run0)
                    k *= 2
                then(dve.tensor_scalar(e_cnt, src[:, TILES - 1, :], float(P - 1), None, ALU.add))
                then(dve.tensor_copy(ints, e_cnt))
                shift = P.bit_length() - 1
                then(dve.tensor_scalar(ints, ints, shift, shift, ALU.arith_shift_right,
                                       ALU.logical_shift_left))
                then(dve.tensor_copy(e_a, ints))
                cur, nxt, k = e_a, e_b, 1
                while k < EXPERTS:
                    then(dve.tensor_copy(nxt[:, 0:k], cur[:, 0:k]))
                    then(dve.tensor_tensor(nxt[:, k:EXPERTS], cur[:, k:EXPERTS], cur[:, 0:EXPERTS - k],
                                           ALU.add))
                    cur, nxt = nxt, (e_c if nxt is e_b else e_b)
                    k *= 2
                then(dve.tensor_tensor(e_base, cur, e_a, ALU.subtract))
                then(dve.tensor_tensor(place, src, total, ALU.subtract))
                then(dve.tensor_tensor(place, place, per_tile(e_base), ALU.add))
                then(dve.tensor_tensor(place, place, PS[:, 0, 0:N].rearrange("p (t e) -> p t e", e=EXPERTS),
                                       ALU.add))
                for mask, slot in ((mask1, self.slot[0]), (mask2, self.slot[1])):
                    then(dve.tensor_tensor(tmp, place, mask, ALU.mult))
                    then(dve.tensor_reduce(pos, tmp, AX.X, ALU.add))
                    then(dve.tensor_copy(slot[:, :], pos))
                then(dve.tensor_tensor(cmp, cur.unsqueeze(1).to_broadcast((P, SLOT_TILES, EXPERTS)),
                                       starts.unsqueeze(2).to_broadcast((P, SLOT_TILES, EXPERTS)),
                                       ALU.is_le))
                then(dve.tensor_reduce(cnt, cmp, AX.X, ALU.add))
                then(dve.tensor_scalar(cnt, cnt, float(EXPERTS - 1), None, ALU.min))
                then(dve.tensor_copy(self.tile_expert[:, :], cnt))
                dve.wait_ge(exp_out, 1)
                then(dve.tensor_scalar(one_plus, ratio, 1.0, None, ALU.add))
                then(dve.reciprocal(self.gate[0][:, :], one_plus))
                then(dve.tensor_tensor(self.gate[1][:, :], self.gate[0][:, :], ratio, ALU.mult))

            @block.tensor
            def _(pe):
                flat = picked.rearrange("p t e -> p (t e)")
                pe.wait_ge(done, 12)
                pe.matmul(PS[:, 0, 0:N], self.tri, flat, start=True, stop=True).then_inc(counted, 1)
                pe.matmul(PS[:, 1, 0:N], self.ones[:, :], flat, start=True, stop=True).then_inc(counted, 1)

            @block.scalar
            def _(act):
                act.wait_ge(exp_in, 1)
                act.activation(ratio, diff, ACT.Exp).then_inc(exp_out, 1)

        with nc.Block() as block:
            @block.gpsimd
            def _(pool):
                for t in range(TILES):
                    for slot in self.slot:
                        pool.indirect_dma_start(
                            self.x_slots, bass.IndirectOffsetOnAxis(ap=slot[:, t:t + 1], axis=0),
                            self.work[:, t, :], None).then_inc(scattered, 16)
                pool.wait_ge(scattered, 16 * 2 * TILES)

    def experts(self, tag):
        nc, PS = self.nc, self.PS
        (loaded0, loaded1, stored0, stored1, xT_done, xT_ready, gate_done, up_done, silu_ready, h_ready,
         hT_done, hT_ready, y_done, y_ready) = (
            self.sem(f"{tag}_e_{n}") for n in
            ("loaded0", "loaded1", "stored0", "stored1", "xT_done", "xT_ready", "gate_done", "up_done",
             "silu_ready", "h_ready", "hT_done", "hT_ready", "y_done", "y_ready"))
        loaded, stored = [loaded0, loaded1], [stored0, stored1]
        xs = self.ring(0, 128)
        xT = self.ring(256, 128)
        sg = self.ring(512, 512)
        hid = self.ring(1536, 512)
        hT = self.ring(2560, 512)
        ys = self.ring(3584, 128)
        XT_BANK, GATE_BANK, UP_BANK, HT_BANK, Y_BANK = 0, 1, 3, 5, 7
        N = SLOT_TILES
        slot_rows = lambda t: bass.ds(t * P, P)

        def stages(t):
            if isinstance(t, int):
                return t < N, 1 <= t <= N, t >= 2
            return True, True, True

        with nc.Block() as block:
            @block.sync
            def _(sp):
                def body(t, u):
                    if not (isinstance(t, int) and t >= N):
                        at_least(sp, xT_done, t - 1)
                        sp.dma_start(xs[u], self.x_slots[slot_rows(t), :]).then_inc(loaded[u], 16)
                    if not (isinstance(t, int) and t < 3):
                        i = t - 3
                        sp.wait_ge(y_ready, i + 1)
                        sp.dma_start(self.y_slots[slot_rows(i), :], ys[1 - u]).then_inc(stored[1 - u], 16)

                pipelined(sp, body, 4, N, N + 3, 2)
                for st in stored:
                    sp.wait_ge(st, 16 * (N // 2))

            @block.tensor
            def _(pe):
                pe.wait_ge(self.experts_loaded, 48)

                def body(t, u):
                    one, two, three = stages(t)
                    if three:
                        i = t - 2
                        pe.wait_ge(h_ready, i + 1)
                        at_least(pe, hT_ready, i - 1)
                        for c in range(CHUNKS):
                            mm = pe.transpose(PS[:, HT_BANK + u, c * P:(c + 1) * P],
                                              hid[u][:, c * P:(c + 1) * P], self.ident)
                        mm.then_inc(hT_done, 1)
                    if one:
                        pe.wait_ge(loaded[u], 8 * (t - u) + 16 if not isinstance(t, int) else 16 * (t // 2) + 16)
                        at_least(pe, xT_ready, t)
                        pe.transpose(PS[:, XT_BANK, 0:P], xs[u], self.ident).then_inc(xT_done, 1)
                    if two:
                        i = t - 1
                        e = pe.value_load(self.tile_expert[0:1, bass.ds(i, 1)], min_val=0, max_val=EXPERTS - 1)
                        pe.wait_ge(xT_ready, i + 1)
                        at_least(pe, silu_ready, i - 1)
                        pe.matmul(PS[:, GATE_BANK + 1 - u, :], xT[1 - u],
                                  self.w_gate[:, bass.ds(e * HIDDEN, HIDDEN)],
                                  start=True, stop=True).then_inc(gate_done, 1)
                        at_least(pe, h_ready, i - 1)
                        pe.matmul(PS[:, UP_BANK + 1 - u, :], xT[1 - u],
                                  self.w_up[:, bass.ds(e * HIDDEN, HIDDEN)],
                                  start=True, stop=True).then_inc(up_done, 1)
                    if three:
                        i = t - 2
                        e = pe.value_load(self.tile_expert[0:1, bass.ds(i, 1)], min_val=0, max_val=EXPERTS - 1)
                        pe.wait_ge(hT_ready, i + 1)
                        at_least(pe, y_ready, i)
                        for c in range(CHUNKS):
                            mm = pe.matmul(PS[:, Y_BANK, 0:D], hT[u][:, c * P:(c + 1) * P],
                                           self.w_down[:, bass.ds(e * (CHUNKS * D) + c * D, D)],
                                           start=(c == 0), stop=(c == CHUNKS - 1))
                        mm.then_inc(y_done, 1)

                pipelined(pe, body, 4, N, N + 2, 2)

            @block.scalar
            def _(act):
                def body(t, u):
                    one, two, three = stages(t)
                    if three:
                        i = t - 2
                        act.wait_ge(hT_done, i + 1)
                        act.activation(hT[u], PS[:, HT_BANK + u, :], ACT.Copy).then_inc(hT_ready, 1)
                    if two:
                        i = t - 1
                        act.wait_ge(gate_done, i + 1)
                        act.activation(sg[1 - u], PS[:, GATE_BANK + 1 - u, :], ACT.Silu)\
                           .then_inc(silu_ready, 1)

                pipelined(act, body, 4, N, N + 2, 2)

            @block.vector
            def _(dve):
                def body(t, u):
                    one, two, three = stages(t)
                    if one:
                        dve.wait_ge(xT_done, t + 1)
                        dve.tensor_copy(xT[u], PS[:, XT_BANK, 0:P]).then_inc(xT_ready, 1)
                    if two:
                        i = t - 1
                        dve.wait_ge(silu_ready, i + 1)
                        dve.wait_ge(up_done, i + 1)
                        dve.tensor_tensor(hid[1 - u], PS[:, UP_BANK + 1 - u, :], sg[1 - u], ALU.mult)\
                           .then_inc(h_ready, 1)
                    if three:
                        i = t - 2
                        at_least(dve, stored[u], 8 * (t - u) - 16 if not isinstance(t, int) else 16 * (i // 2))
                        dve.wait_ge(y_done, i + 1)
                        dve.tensor_copy(ys[u], PS[:, Y_BANK, 0:D]).then_inc(y_ready, 1)

                pipelined(dve, body, 4, N, N + 2, 2)

    def combine(self, tag, store):
        nc = self.nc
        DEEP = 4
        gathered = [self.sem(f"{tag}_c_gathered{i}") for i in range(DEEP)]
        half_done, x_done, out_done = (self.sem(f"{tag}_c_{n}") for n in ("half_done", "x_done", "out_done"))
        y = [[self.scratch[:, (2 * i + k) * D:(2 * i + k + 1) * D] for k in range(2)] for i in range(DEEP)]
        with nc.Block() as block:
            @block.gpsimd
            def _(pool):
                for t in range(TILES):
                    at_least(pool, x_done, t - DEEP + 1)
                    for k in range(2):
                        pool.indirect_dma_start(
                            y[t % DEEP][k], None, self.y_slots,
                            bass.IndirectOffsetOnAxis(ap=self.slot[k][:, t:t + 1], axis=0))\
                            .then_inc(gathered[t % DEEP], 16)

            @block.vector
            def _(dve):
                for t in range(TILES):
                    dve.wait_ge(gathered[t % DEEP], 32 * (t // DEEP + 1))
                    for k, step in enumerate((half_done, x_done)):
                        dve.scalar_tensor_tensor(out=self.X[:, t, :], in0=y[t % DEEP][k],
                                                 scalar=self.gate[k][:, t:t + 1], in1=self.X[:, t, :],
                                                 op0=ALU.mult, op1=ALU.add).then_inc(step, 1)
                        if k == 0:
                            dve.wait_ge(half_done, t + 1)

            if store:
                @block.sync
                def _(sp):
                    out = self.dram["out"].rearrange("(t p) d -> p t d", p=P)
                    for i in range(ROUNDS):
                        sp.wait_ge(x_done, QUAD * (i + 1))
                        sp.dma_start(out[:, QUAD * i:QUAD * (i + 1), :],
                                     self.X[:, QUAD * i:QUAD * (i + 1), :]).then_inc(out_done, 16)
                    sp.wait_ge(out_done, 16 * ROUNDS)


def build(nc, dram):
    with ExitStack() as ctx:
        k = Hybrid(nc, ctx, dram)
        k.setup()
        k.project("a", rotary=False)
        k.attend("a_s", causal=False)
        k.finish("a")
        k.route("a")
        k.experts("a")
        k.combine("a", store=False)
        k.project("b", rotary=True)
        k.attend("b_s", causal=True)
        k.finish("b")
        k.route("b")
        k.experts("b")
        k.combine("b", store=True)


def constants():
    p = np.arange(P)
    keep = np.zeros((P, C_KEEP), np.float32)
    keep[:, C_IDENT:C_IDENT + P] = np.eye(P)
    keep[:, C_TRI:C_TRI + P] = p[:, None] < p[None, :]
    freqs = np.float32(THETA) ** (-np.arange(0, DH, 2, dtype=np.float32) / np.float32(DH))
    angle = np.arange(S, dtype=np.float32)[None, :] * freqs[(p % DH) // 2][:, None]
    keep[:, C_COS:C_COS + S] = np.cos(angle)
    keep[:, C_SIN:C_SIN + S] = np.sin(angle) * np.where(p % 2 == 0, -1, 1)[:, None]
    keep[:, C_KBIAS] = p % ROW == SHIFT_ROW
    keep[:, C_RANK:C_RANK + EXPERTS] = EXPERTS - np.arange(EXPERTS)
    keep[:, C_START:C_START + SLOT_TILES] = np.arange(SLOT_TILES) * P
    staged = np.zeros((P, C_STAGED), np.float32)
    for a in range(2):
        row, col = a * P + p[:, None], np.arange(S)[None, :]
        staged[:, a * S:(a + 1) * S] = np.where(col > row, MASKED, 0)
        staged[:, (2 + a) * S:(3 + a) * S] = np.where(row > col, MASKED, 0)
    for n, blocks in enumerate(((0, 1), (2,), (0, 2), (1,))):
        for g in range(GROUPS):
            for j in range(QUAD):
                for b in blocks:
                    for d in range(DH):
                        staged[DH * (QUAD * g + j) + d,
                               C_PERM + (n * GROUPS + g) * P + ROW * j + DH * b + d] = 1
    return keep, staged


def kernel(**inputs):
    import concourse.bacc as _bacc
    from concourse.bass_utils import run_bass_kernel_spmd as _run

    a = {n: np.asarray(v) for n, v in inputs.items()}
    c = np.ascontiguousarray
    keep, staged = constants()
    swap = np.arange(D) ^ 1
    A, Bn, Fn = "L0_attn_a_", "L0_attn_b_", "L0_ffn_"
    arrays = {
        "x": c(a[A + "x"].reshape(TOKENS, D)),
        "consts": keep, "staged": staged,
        "w_a_q": c(a[A + "Wq"].T), "w_a_k": c(a[A + "Wk"].T), "w_a_v": c(a[A + "Wv"].T),
        "w_a_o": c(a[A + "Wff"].T),
        "w_b_q": c(a[Bn + "Wq"].T), "w_b_k": c(a[Bn + "Wk"].T), "w_b_v": c(a[Bn + "Wv"].T),
        "w_b_qs": c(a[Bn + "Wq"][swap].T), "w_b_ks": c(a[Bn + "Wk"][swap].T), "w_b_o": c(a[Bn + "Wo"].T),
        "bias_q": a[Bn + "bq"], "bias_k": a[Bn + "bk"], "bias_qs": c(a[Bn + "bq"][swap]),
        "bias_ks": c(a[Bn + "bk"][swap]), "bias_scale": a[Bn + "scale"],
        "rows_a_o": a[A + "bff"], "rows_b_v": a[Bn + "bv"], "rows_b_o": a[Bn + "bo"],
        "w_route": c(a[Fn + "wg"].T), "b_route": a[Fn + "bg"],
        "w_gate": c(a[Fn + "Wgate"].transpose(2, 0, 1).reshape(D, EXPERTS * HIDDEN)),
        "w_up": c(a[Fn + "Wup"].transpose(2, 0, 1).reshape(D, EXPERTS * HIDDEN)),
        "w_down": c(a[Fn + "Wdown"].reshape(EXPERTS, D, CHUNKS, P).transpose(3, 0, 2, 1)
                    .reshape(P, EXPERTS * CHUNKS * D)),
    }
    from concourse import mybir as _mybir
    nc = _bacc.Bacc("TRN2", target_bir_lowering=False, num_devices=1)
    dram = {n: nc.dram_tensor(f"in_{n}", v.shape, _mybir.dt.from_np(v.dtype), kind="ExternalInput").ap()
            for n, v in arrays.items()}
    dram["out"] = nc.dram_tensor("out", (TOKENS, D), F32, kind="ExternalOutput").ap()
    build(nc, dram)
    r = _run(nc, [{f"in_{n}": v for n, v in arrays.items()}], core_ids=[0])
    return r.results[0]["out"].reshape(B, S, D)
```

```python
from contextlib import ExitStack

import numpy as np
import concourse.bass as bass
from concourse import mybir

F32 = mybir.dt.float32
F32R = mybir.dt.float32r
BF16 = mybir.dt.bfloat16
I32 = mybir.dt.int32
ACT = mybir.ActivationFunctionType
ALU = mybir.AluOpType
AX = mybir.AxisListType

B, S, D = 16, 256, 128
HEADS = 16
DH = D // HEADS
TOKENS = B * S
P = 128
TILES = TOKENS // P
QUAD = 4
GROUPS = HEADS // QUAD
HALVES = 2
H_TOKENS = TOKENS // HALVES
H_TILES = TILES // HALVES
STEPS = B * GROUPS // HALVES
ROUNDS = H_TILES // QUAD
ROW = 32
SHIFT_ROW = 3 * DH
EXPERTS = 8
HIDDEN = 512
CHUNKS = HIDDEN // P
SLOT_TILES = 2 * H_TILES + EXPERTS
EPS = 1e-5
AHEAD = 2
MASKED = -100000.0
THETA = 10000.0
Q_SCALE_A = float(1.0 / np.sqrt(np.float32(D)))
BIG = 3.0e38

C_IDENT = 0
C_TRI = C_IDENT + P
C_COS = C_TRI + P
C_SIN = C_COS + S
C_KBIAS = C_SIN + S
C_RANK = C_KBIAS + 1
C_START = C_RANK + EXPERTS
C_QMASK = C_START + SLOT_TILES
C_KEEP = C_QMASK + 2 * P
C_KMASK = 0
C_PERM = 2 * P
N_PERM = 4 * GROUPS * P
C_STAGED = C_PERM + N_PERM


def at_least(engine, semaphore, value):
    if not (isinstance(value, int) and value <= 0):
        engine.wait_ge(semaphore, value)


def pipelined(engine, body, first, n, steps, unroll):
    assert first % unroll == 0 and (n - first) % unroll == 0
    for t in range(first):
        body(t, t % unroll)
    with engine.Fori(0, (n - first) // unroll) as turn:
        for u in range(unroll):
            body(turn * unroll + (first + u), u)
    for t in range(n, steps):
        body(t, t % unroll)


class Hybrid:

    def __init__(self, nc, ctx, dram):
        self.nc, self.ctx, self.dram, self.used = nc, ctx, dram, []
        sb = self.sb
        self.X = sb("X", [P, TILES, D])
        self.work = sb("work", [P, TILES, D])
        self.q_hi = sb("q_hi", [P, H_TOKENS], F32R)
        self.q_lo = sb("q_lo", [P, H_TOKENS], F32R)
        self.k_hi = sb("k_hi", [P, H_TOKENS], F32R)
        self.k_lo = sb("k_lo", [P, H_TOKENS], F32R)
        self.w_gate = [sb(f"w_gate_{n}", [P, EXPERTS * HIDDEN], F32R) for n in ("hi", "lo")]
        self.w_up = [sb(f"w_up_{n}", [P, EXPERTS * HIDDEN], F32R) for n in ("hi", "lo")]
        self.w_down = sb("w_down", [P, EXPERTS * CHUNKS * D])
        self.scratch = sb("scratch", [P, 4096])
        self.consts = sb("consts", [P, C_KEEP])
        self.perm = sb("perm", [P, N_PERM], F32R)
        self.key_mask = sb("key_mask", [P, 2 * P], BF16)
        self.ident_b = sb("ident_b", [P, P], BF16)
        self.ones = sb("ones", [P, P])
        self.eps4 = sb("eps4", [P, 1])
        self.stack = [sb(f"stack{i}", [P, 2 * S], F32R) for i in range(GROUPS)]
        self.q_shifted = [sb(f"q_shifted{i}", [P, S], F32R) for i in range(2)]
        self.row_max = [sb(f"row_max{i}", [P, 2, QUAD, ROW]) for i in range(2)]
        self.v_ones = [sb(f"v_ones{g}", [P, 2, QUAD, ROW]) for g in range(GROUPS)]
        self.out_t = [sb(f"out_t{i}", [P, S]) for i in range(2)]
        self.junk = self.sb("junk", [P, QUAD, P + S], BF16)
        self.y_rows = sb("y_rows", [P, 8 * D])
        self.rec_den = sb("rec_den", [P, 2, QUAD])
        self.logits = sb("logits", [P, TILES, EXPERTS])
        self.slot = [sb(f"slot{i}", [P, TILES], I32) for i in range(2)]
        self.gate = [sb(f"gate{i}", [P, TILES]) for i in range(2)]
        self.tile_cols = [sb(f"tile_cols{h}", [P, SLOT_TILES + 2 * AHEAD + 2], I32) for h in range(HALVES)]
        self.stats = sb("stats", [P, QUAD, 6])
        self.mean_var = [sb(f"mean_var{i}", [P, QUAD, 2]) for i in range(2)]
        self.root = [sb(f"root{i}", [P, QUAD]) for i in range(2)]
        self.carrier = sb("carrier", [P, QUAD])
        self.inv = sb("inv", [P, QUAD])
        self.inv2 = sb("inv2", [P, QUAD])
        self.rstd = [sb(f"rstd{i}", [P, QUAD]) for i in range(2)]
        self.w_att = {n: sb(f"w_{n}", [P, D]) for n in
                      ("a_q", "a_k", "a_v", "a_o", "b_q", "b_k", "b_qs", "b_ks", "b_v", "b_o")}
        self.bias = {n: sb(f"bias_{n}", [P, 1]) for n in ("q", "k", "qs", "ks", "scale")}
        self.rows = {n: sb(f"rows_{n}", [P, D]) for n in ("a_o", "b_v", "b_o")}
        self.w_route = sb("w_route", [P, EXPERTS])
        self.b_route = sb("b_route", [P, EXPERTS])
        self.PS = ctx.enter_context(nc.psum_tensor("PS", [P, 8, 512], F32))
        self.x_slots, self.y_slots = (
            [nc.dram_tensor(f"{n}_slots{h}", (SLOT_TILES * P, D), F32, kind="Internal").ap()
             for h in range(HALVES)] for n in "xy")
        self.ident = self.consts[:, C_IDENT:C_IDENT + P]
        self.tri = self.consts[:, C_TRI:C_TRI + P]
        self.q_mask = self.consts[:, C_QMASK:C_QMASK + 2 * P]

    def sb(self, name, shape, dt=F32):
        return self.ctx.enter_context(self.nc.sbuf_tensor(name, shape, dt))

    def sem(self, name):
        self.used.append(self.nc.alloc_semaphore(name))
        return self.used[-1]

    def fresh_semaphores(self):
        self.nc.clear_and_free_semaphores(self.used)
        self.nc.all_engine_barrier()
        self.used = []

    def setup(self):
        nc, d = self.nc, self.dram
        loaded, staged, cleared, zeroed, ones_set, hi_ready, lo_ready, small = (
            self.sem(n) for n in ("const_loaded", "staged", "cleared", "zeroed", "ones_set", "hi_ready",
                                  "lo_ready", "small_loaded"))
        table = self.scratch[:, 0:C_STAGED]
        W = EXPERTS * HIDDEN
        lower = self.work[:, :, :].rearrange("p t d -> p (t d)")
        upper = self.X[:, TILES // 2:, :].rearrange("p t d -> p (t d)")
        pieces = [(lower[:, 0:W // 2], self.w_gate, "w_gate", slice(0, W // 2)),
                  (lower[:, W // 2:W], self.w_gate, "w_gate", slice(W // 2, W)),
                  (upper, self.w_up, "w_up", slice(0, W // 2)),
                  (lower[:, 0:W // 2], self.w_up, "w_up", slice(W // 2, W))]
        raw = [self.sem(f"raw_loaded{i}") for i in range(len(pieces))]
        x = d["x"].rearrange("(t p) d -> p t d", p=P)
        n_loads = 4 + len(self.w_att)
        with nc.Block() as block:
            @block.sync
            def _(sp):
                for i in range(3):
                    sp.dma_start(pieces[i][0], d[pieces[i][2]][:, pieces[i][3]]).then_inc(raw[i], 16)
                sp.dma_start(table, d["staged"]).then_inc(staged, 16)
                sp.dma_start(self.consts[:, :], d["consts"]).then_inc(loaded, 16)
                sp.dma_start(self.X[:, 0:H_TILES, :], x[:, 0:H_TILES, :]).then_inc(loaded, 16)
                for n, w in self.w_att.items():
                    sp.dma_start(w[:, :], d[f"w_{n}"]).then_inc(loaded, 16)
                sp.dma_start(self.w_route[:, :], d["w_route"]).then_inc(loaded, 16)
                sp.dma_start(self.w_down[:, :], d["w_down"]).then_inc(loaded, 16)
                sp.wait_ge(lo_ready, 1)
                sp.dma_start(pieces[3][0], d[pieces[3][2]][:, pieces[3][3]]).then_inc(raw[3], 16)
                sp.wait_ge(cleared, 1)
                blank = self.row_max[0][:, :, :, :].rearrange("p q j r -> p (q j r)")
                for h in range(HALVES):
                    rows = self.x_slots[h].rearrange("(p c r) d -> p c (r d)", p=P, r=2)
                    sp.dma_start(rows, blank.unsqueeze(1).to_broadcast((P, SLOT_TILES // 2, 2 * D)))\
                      .then_inc(zeroed, 16)
                sp.wait_ge(lo_ready, 3)
                sp.dma_start(self.X[:, H_TILES:, :], x[:, H_TILES:, :]).then_inc(loaded, 16)
                sp.wait_ge(loaded, 16 * (n_loads + 1))
                sp.wait_ge(zeroed, 16 * HALVES)

            @block.scalar
            def _(act):
                n = 0
                for name, b in self.bias.items():
                    src = d[f"bias_{name}"]
                    if name == "scale":
                        src = src.rearrange("(o n) -> o n", o=1).to_broadcast((P, 1))
                    else:
                        src = src.rearrange("(p o) -> p o", o=1)
                    act.dma_start(b[:, :], src).then_inc(small, 16)
                    n += 16
                for name, r in self.rows.items():
                    act.dma_start(r[:, :], d[f"rows_{name}"].rearrange("(o n) -> o n", o=1)
                                  .to_broadcast((P, D))).then_inc(small, 16)
                    n += 16
                act.dma_start(self.b_route[:, :], d["b_route"].rearrange("(o n) -> o n", o=1)
                              .to_broadcast((P, EXPERTS))).then_inc(small, 16)
                for i, (at, parts, _, cols) in enumerate(pieces):
                    act.wait_ge(raw[i], 16)
                    act.activation(parts[0][:, cols], at, ACT.Copy).then_inc(hi_ready, 1)
                act.wait_ge(small, n + 16)

            @block.gpsimd
            def _(pool):
                for i in range(2):
                    pool.memset(self.row_max[i][:, :, :, :], 0.0).then_inc(cleared, 1)
                for g in range(GROUPS):
                    pool.memset(self.v_ones[g][:, :, :, :], 0.0).then_inc(ones_set, 1)
                    pool.wait_ge(ones_set, g + 1)
                    pool.memset(self.v_ones[g][:, :, :, DH:DH + 1], 1.0)
                pool.memset(self.ones[:, :], 1.0)
                pool.memset(self.eps4[:, :], EPS / 4)
                for cols in self.tile_cols:
                    pool.memset(cols[:, :], 0)

            @block.vector
            def _(dve):
                for i, (at, parts, _, cols) in enumerate(pieces):
                    dve.wait_ge(hi_ready, i + 1)
                    dve.tensor_tensor(parts[1][:, cols], at, parts[0][:, cols].bitcast(F32), ALU.subtract)\
                       .then_inc(lo_ready, 1)
                dve.wait_ge(staged, 16)
                dve.tensor_copy(self.perm[:, :], table[:, C_PERM:C_PERM + N_PERM])
                dve.tensor_copy(self.key_mask[:, :], table[:, C_KMASK:C_KMASK + 2 * P])
                dve.wait_ge(loaded, 16 * n_loads)
                dve.tensor_copy(self.ident_b[:, :], self.ident)

    def norm_sems(self, tag):
        return {n: self.sem(f"{tag}_{n}") for n in
                ("stats_done", "var_done", "root_done", "newton_done", "xn_done")}

    def carry_wait(self, dve, j=0):
        dve.memset(self.carrier[:, j:j + 1], 0.0)

    def norm_stats(self, dve, i, u, s, base):
        self.carry_wait(dve)
        for j in range(QUAD):
            dve.bn_stats(self.stats[:, j, :], self.X[:, base + QUAD * i + j, :]).then_inc(s["stats_done"], 1)
        dve.wait_ge(s["stats_done"], QUAD * i + QUAD)
        self.carry_wait(dve)
        for j in range(QUAD):
            dve.bn_aggr(self.mean_var[u][:, j, :], self.stats[:, j, :]).then_inc(s["var_done"], 1)

    def norm_root(self, act, i, u, s):
        act.wait_ge(s["var_done"], QUAD * i + QUAD)
        act.activation(self.root[u][:, :], self.mean_var[u][:, :, 1], ACT.Sqrt,
                       bias=self.eps4[:, :], scale=0.25).then_inc(s["root_done"], 1)

    def norm_rows(self, dve, i, u, s, xn, base):
        dve.wait_ge(s["root_done"], i + 1)
        step = s["newton_done"]
        dve.reciprocal(self.inv[:, :], self.root[u][:, :]).then_inc(step, 1)
        dve.tensor_scalar(self.inv2[:, :], self.mean_var[u][:, :, 1], EPS, 0.25, ALU.add,
                          ALU.mult).then_inc(step, 1)
        dve.wait_ge(step, 5 * i + 2)
        dve.tensor_tensor(self.inv2[:, :], self.inv2[:, :], self.inv[:, :], ALU.mult).then_inc(step, 1)
        dve.wait_ge(step, 5 * i + 3)
        dve.tensor_tensor(self.inv[:, :], self.inv2[:, :], self.root[u][:, :], ALU.add).then_inc(step, 1)
        dve.wait_ge(step, 5 * i + 4)
        dve.reciprocal(self.rstd[u][:, :], self.inv[:, :]).then_inc(step, 1)
        dve.wait_ge(step, 5 * i + 5)
        for j in range(QUAD):
            dve.tensor_scalar(xn[:, j, :], self.X[:, base + QUAD * i + j, :], self.mean_var[u][:, j, 0:1],
                              self.rstd[u][:, j:j + 1], ALU.subtract, ALU.mult).then_inc(s["xn_done"], 1)

    def ring(self, at, n, *dims):
        out = []
        for i in range(2):
            v = self.scratch[:, at + i * n:at + (i + 1) * n]
            if dims:
                v = v.rearrange("p (t d) -> p t d", t=dims[0])
            out.append(v)
        return out

    def project(self, tag, half, rotary, pool_job=None):
        nc, PS = self.nc, self.PS
        base = half * H_TILES
        s = self.norm_sems(tag)
        xT_done, xT_ready, proj_done, v_done, hi_ready, rot_done, qk_used, v_used = (
            self.sem(f"{tag}_{n}") for n in ("xT_done", "xT_ready", "proj_done", "v_done", "hi_ready",
                                             "rot_done", "qk_used", "v_used"))
        xn = self.ring(0, 512, QUAD)
        xT = self.ring(1024, 512)
        turned = [self.scratch[:, 2048 + 512 * i:2560 + 512 * i] for i in range(2)]
        part = [self.scratch[:, 3072 + 512 * i:3584 + 512 * i] for i in range(2)]
        kinds = ("q", "k", "qs", "ks") if rotary else ("q", "k")
        L = "b" if rotary else "a"
        T_BANK, V_BANK = 0, 7
        bank = {"q": 1, "k": 2, "qs": 3, "ks": 4}
        hi = {"q": self.q_hi, "k": self.k_hi}
        lo = {"q": self.q_lo, "k": self.k_lo}
        cols = lambda i: bass.ds(i * 512, 512)

        with nc.Block() as block:
            if pool_job is not None:
                block.gpsimd(pool_job)

            @block.vector
            def _(dve):
                def rotate(i):
                    for n, kind in enumerate(("q", "k")):
                        at_least(dve, rot_done, 6 * i + 3 * n)
                        for m, (src, trig) in enumerate(((kind, C_COS), (kind + "s", C_SIN))):
                            dve.wait_ge(proj_done, len(kinds) * i + kinds.index(src) + 1)
                            dve.scalar_tensor_tensor(
                                out=part[m].rearrange("p (b s) -> p b s", b=2),
                                in0=PS[:, bank[src], :].rearrange("p (b s) -> p b s", b=2),
                                scalar=self.bias[src][:, 0:1],
                                in1=self.consts[:, trig:trig + S].unsqueeze(1).to_broadcast((P, 2, S)),
                                op0=ALU.add, op1=ALU.mult).then_inc(rot_done, 1)
                        dve.wait_ge(rot_done, 6 * i + 3 * n + 2)
                        at_least(dve, qk_used, 2 * i + n - 1)
                        dve.tensor_tensor(turned[n], part[0], part[1], ALU.add)\
                           .then_inc(rot_done, 1)

                def low_parts(i):
                    for n, kind in enumerate(("q", "k")):
                        dve.wait_ge(hi_ready, 2 * i + n + 1)
                        value = turned[n] if rotary else PS[:, bank[kind], :]
                        scale = (self.bias["scale"][:, 0:1] if rotary else Q_SCALE_A) if kind == "q" else 1.0
                        dve.scalar_tensor_tensor(out=lo[kind][:, cols(i)], in0=value, scalar=scale,
                                                 in1=hi[kind][:, cols(i)].bitcast(F32), op0=ALU.mult,
                                                 op1=ALU.subtract).then_inc(qk_used, 1)

                def body(t, u):
                    if not (isinstance(t, int) and t >= ROUNDS):
                        self.norm_stats(dve, t, u, s, base)
                    if not (isinstance(t, int) and t < 1):
                        i = t - 1
                        if rotary:
                            rotate(i)
                        low_parts(i)
                        if rotary:
                            dve.wait_ge(v_done, i + 1)
                            dve.tensor_tensor(self.work[:, bass.ds(QUAD * i + base, QUAD), :],
                                              PS[:, V_BANK, :].rearrange("p (t d) -> p t d", t=QUAD),
                                              self.rows["b_v"][:, :].unsqueeze(1).to_broadcast((P, QUAD, D)),
                                              ALU.add).then_inc(v_used, 1)
                    if not (isinstance(t, int) and t >= ROUNDS):
                        self.norm_rows(dve, t, u, s, xn[u], base)

                pipelined(dve, body, 2, ROUNDS, ROUNDS + 1, 2)

            @block.tensor
            def _(pe):
                def body(i, u):
                    pe.wait_ge(s["xn_done"], QUAD * i + QUAD)
                    at_least(pe, xT_ready, i)
                    for j in range(QUAD):
                        mm = pe.transpose(PS[:, T_BANK, j * P:(j + 1) * P], xn[u][:, j, :], self.ident)
                    mm.then_inc(xT_done, 1)
                    pe.wait_ge(xT_ready, i + 1)
                    at_least(pe, qk_used, 2 * i)
                    for kind in kinds:
                        pe.matmul(PS[:, bank[kind], :], self.w_att[f"{L}_{kind}"][:, :], xT[u],
                                  start=True, stop=True).then_inc(proj_done, 1)
                    at_least(pe, v_used, i)
                    for j in range(QUAD):
                        mm = pe.matmul(PS[:, V_BANK, j * D:(j + 1) * D], xT[u][:, j * P:(j + 1) * P],
                                       self.w_att[f"{L}_v"][:, :], start=True, stop=True)
                    mm.then_inc(v_done, 1)

                pipelined(pe, body, 2, ROUNDS, ROUNDS, 2)

            @block.scalar
            def _(act):
                def body(t, u):
                    if not (isinstance(t, int) and t >= ROUNDS):
                        self.norm_root(act, t, u, s)
                    if not (isinstance(t, int) and t < 1):
                        i = t - 1
                        for n, kind in enumerate(("q", "k")):
                            if rotary:
                                act.wait_ge(rot_done, 6 * i + 3 * n + 3)
                            else:
                                act.wait_ge(proj_done, 2 * i + n + 1)
                            value = turned[n] if rotary else PS[:, bank[kind], :]
                            scale = (self.bias["scale"][:, 0:1] if rotary else Q_SCALE_A) if kind == "q" else 1.0
                            act.activation(hi[kind][:, cols(i)], value, ACT.Copy, scale=scale)\
                               .then_inc(hi_ready, 1)
                        if not rotary:
                            act.wait_ge(v_done, i + 1)
                            act.activation(self.work[:, bass.ds(QUAD * i + base, QUAD), :],
                                           PS[:, V_BANK, :].rearrange("p (t d) -> p t d", t=QUAD),
                                           ACT.Copy).then_inc(v_used, 1)
                    if not (isinstance(t, int) and t >= ROUNDS):
                        act.wait_ge(xT_done, t + 1)
                        act.activation(xT[u], PS[:, T_BANK, :], ACT.Copy).then_inc(xT_ready, 1)

                pipelined(act, body, 2, ROUNDS, ROUNDS + 1, 2)

    def attend(self, tag, half, causal):
        nc, PS = self.nc, self.PS
        base = half * H_TILES
        (stack_done, stack_ready, score_done, max_ready, shift_done, q_ready, scoreT_done, probs_ready,
         pv_done, outT_ready, out_done, rec_ready, out_used, v_ready) = (
            self.sem(f"{tag}_{n}") for n in
            ("stack_done", "stack_ready", "score_done", "max_ready", "shift_done", "q_ready",
             "scoreT_done", "probs_ready", "pv_done", "outT_ready", "out_done", "rec_ready",
             "out_used", "v_ready"))
        probs = [self.scratch[:, 2048 * i:2048 * (i + 1)].rearrange("p (j n) -> p j n", j=QUAD)
                 for i in range(2)]
        KEYS_BANK, SCORE_BANK, PV_BANK, STACK_BANK = 0, 4, 6, 7
        per_head = 2 if causal else 1
        left = P if causal else 0

        def exists(t, late):
            return not isinstance(t, int) or 0 <= t - late < STEPS

        with nc.Block() as block:
            @block.tensor
            def _(pe):
                def stack_parts(t, g):
                    at_least(pe, stack_ready, 2 * t)
                    at_least(pe, q_ready, t - 1)
                    tokens = bass.ds((t - g) * (S // GROUPS), S)
                    for n, parts in enumerate(((self.q_hi, self.q_lo), (self.k_hi, self.k_lo))):
                        for m, part in enumerate(parts):
                            c = ((2 * n + m) * GROUPS + g) * P
                            mm = pe.matmul(PS[:, STACK_BANK, n * S:(n + 1) * S], self.perm[:, c:c + P],
                                           part[:, tokens], start=(m == 0), stop=(m == 1))
                    mm.then_inc(stack_done, 1)

                def scores(s, g, j):
                    at_least(pe, max_ready, per_head * (QUAD * s + j - 1))
                    out = PS[:, SCORE_BANK + j % 2, :]
                    r = slice(ROW * j, ROW * j + ROW)
                    for q in range(2):
                        mm = pe.matmul(out[:, q * S:(q + 1) * S], self.stack[g][r, q * P:(q + 1) * P],
                                       self.stack[g][r, S:2 * S], start=True, stop=True,
                                       skip_group_check=True)
                    mm.then_inc(score_done, 1)

                def shifts(s, g):
                    pe.wait_ge(max_ready, per_head * QUAD * (s + 1))
                    for q in range(2):
                        mm = pe.transpose(PS[:, STACK_BANK, q * P:(q + 1) * P],
                                          self.row_max[g % 2][:, q, :, :].rearrange("p j r -> p (j r)"),
                                          self.ident)
                    mm.then_inc(shift_done, 1)

                def scores_t(s, g, part):
                    at_least(pe, probs_ready, 2 * s + part - 1)
                    for j in (2 * part, 2 * part + 1):
                        out = PS[:, KEYS_BANK + j, :]
                        r = slice(ROW * j, ROW * j + ROW)
                        for k in range(2):
                            at = (1 - k) * S
                            mm = pe.matmul(out[:, at:at + S], self.stack[g][r, S + k * P:S + (k + 1) * P],
                                           self.q_shifted[g % 2][r, :], start=(k == 0),
                                           stop=(k == 1 and not causal), skip_group_check=True)
                        if causal:
                            mm = pe.matmul(out[:, P:3 * P], self.ident_b[:, :], self.key_mask[:, :],
                                           start=False, stop=True, skip_group_check=True)
                    mm.then_inc(scoreT_done, 1)

                def products(s, g):
                    for k in range(2):
                        skip = left if k == 1 else 0
                        at = (1 - k) * S + skip
                        for j in range(QUAD):
                            mm = pe.matmul(PS[ROW * j:ROW * j + ROW, PV_BANK, skip:S],
                                           self.v_ones[g][:, k, j, :], probs[g % 2][:, j, at:at + S - skip],
                                           start=(k == 0), stop=(k == 1), skip_group_check=True)
                    mm.then_inc(pv_done, 1)

                def body(t, g):
                    g1, g2, g3 = ((g - late) % GROUPS for late in (1, 2, 3))
                    if exists(t, 2):
                        if exists(t, 1):
                            pe.wait_ge(stack_ready, 2 * t)
                        shifts(t - 2, g2)
                    if exists(t, 1):
                        pe.wait_ge(stack_ready, 2 * t)
                        scores(t - 1, g1, 0)
                    if exists(t, 3):
                        pe.wait_ge(q_ready, t - 2)
                        scores_t(t - 3, g3, 0)
                    if exists(t, 1):
                        scores(t - 1, g1, 1)
                    if exists(t, 5):
                        pe.wait_ge(outT_ready, t - 4)
                        for q in range(2):
                            mm = pe.transpose(PS[:, PV_BANK, S + q * P:S + (q + 1) * P],
                                              self.out_t[g1 % 2][:, q * P:(q + 1) * P], self.ident)
                        mm.then_inc(out_done, 1)
                    if exists(t, 1):
                        scores(t - 1, g1, 2)
                    if exists(t, 3):
                        scores_t(t - 3, g3, 1)
                    if exists(t, 0):
                        stack_parts(t, g)
                    if exists(t, 1):
                        scores(t - 1, g1, 3)
                    if exists(t, 4):
                        pe.wait_ge(probs_ready, 2 * (t - 3))
                        pe.wait_ge(v_ready, t - 3)
                        at_least(pe, out_used, t - 4)
                        products(t - 4, g)

                pipelined(pe, body, 8, STEPS, STEPS + 5, 4)

            @block.scalar
            def _(act):
                def body(t, g):
                    if exists(t, 5):
                        act.wait_ge(pv_done, t - 4)
                        at_least(act, out_done, t - 6)
                        act.activation(self.out_t[(g - 1) % 2][:, :], PS[:, PV_BANK, 0:S], ACT.Copy)\
                           .then_inc(outT_ready, 1)
                    if exists(t, 3):
                        s = t - 3
                        for part in range(2):
                            act.wait_ge(scoreT_done, 2 * s + part + 1)
                            at_least(act, pv_done, s - 1)
                            act.activation(probs[(g - 3) % 2][:, 2 * part:2 * part + 2, left:2 * S],
                                           PS[:, KEYS_BANK + 2 * part:KEYS_BANK + 2 * part + 2, left:2 * S],
                                           ACT.Exp).then_inc(probs_ready, 1)
                    if exists(t, 0):
                        act.wait_ge(stack_done, t + 1)
                        at_least(act, scoreT_done, 2 * (t - 3))
                        act.activation(self.stack[g][:, 0:S], PS[:, STACK_BANK, 0:S], ACT.Copy)\
                           .then_inc(stack_ready, 1)
                        act.activation(self.stack[g][:, S:2 * S], PS[:, STACK_BANK, S:2 * S], ACT.Identity,
                                       bias=self.consts[:, C_KBIAS:C_KBIAS + 1]).then_inc(stack_ready, 1)

                pipelined(act, body, 8, STEPS, STEPS + 5, 4)

            @block.vector
            def _(dve):
                def maxima(s, g, j):
                    dve.wait_ge(score_done, QUAD * s + j + 1)
                    out = PS[:, SCORE_BANK + j % 2, :]
                    to = self.row_max[g % 2]
                    if not causal:
                        dve.tensor_reduce(to[:, :, j, SHIFT_ROW:SHIFT_ROW + 1],
                                          out.rearrange("p (q k) -> p q k", q=2),
                                          AX.X, ALU.max).then_inc(max_ready, 1)
                        return
                    self.carry_wait(dve, j)
                    junk = self.junk[:, j, :]
                    dve.tensor_tensor_reduce(junk[:, 0:P], out[:, 0:P], self.q_mask[:, P:2 * P], 1.0, -BIG,
                                             ALU.add, ALU.max, to[:, 0, j, SHIFT_ROW:SHIFT_ROW + 1])\
                       .then_inc(max_ready, 1)
                    dve.tensor_tensor_reduce(junk[:, P:P + S], out[:, S:2 * S], self.q_mask, 1.0, -BIG, ALU.add,
                                             ALU.max, to[:, 1, j, SHIFT_ROW:SHIFT_ROW + 1])\
                       .then_inc(max_ready, 1)

                def body(t, g):
                    g1, g2 = ((g - late) % GROUPS for late in (1, 2))
                    if exists(t, 2):
                        dve.wait_ge(shift_done, t - 1)
                        dve.tensor_tensor(self.q_shifted[g % 2][:, :], self.stack[g2][:, 0:S].bitcast(F32),
                                          PS[:, STACK_BANK, 0:S], ALU.subtract).then_inc(q_ready, 1)
                    if exists(t, 1):
                        maxima(t - 1, g1, 0)
                        maxima(t - 1, g1, 1)
                    if exists(t, 5):
                        s = t - 5
                        dve.wait_ge(out_done, s + 1)
                        rows = PS[:, PV_BANK, S:2 * S].rearrange("p (q j r) -> p q j r", q=2, j=QUAD)
                        dve.reciprocal(self.rec_den[:, :, :], rows[:, :, :, DH]).then_inc(rec_ready, 1)
                        dve.wait_ge(rec_ready, s + 1)
                        batch2 = (s - g1) // 2 if isinstance(s, int) else (t - (g1 + 5)) // 2
                        out = self.work[:, bass.ds(batch2 + base, 2), ROW * g1:ROW * g1 + ROW]\
                            .rearrange("p q (j d) -> p q j d", j=QUAD)
                        dve.tensor_tensor(out, rows[:, :, :, 0:DH],
                                          self.rec_den[:, :, :].unsqueeze(3).to_broadcast((P, 2, QUAD, DH)),
                                          ALU.mult).then_inc(out_used, 1)
                    if exists(t, 1):
                        maxima(t - 1, g1, 2)
                        maxima(t - 1, g1, 3)

                pipelined(dve, body, 8, STEPS, STEPS + 5, 4)

            @block.gpsimd
            def _(pool):
                def body(s, g):
                    at_least(pool, pv_done, s - 3)
                    tiles = bass.ds((s - g) // 2 + base, 2)
                    pool.tensor_copy(self.v_ones[g][:, :, :, 0:DH],
                                     self.work[:, tiles, ROW * g:ROW * g + ROW]
                                     .rearrange("p q (j d) -> p q j d", j=QUAD)).then_inc(v_ready, 1)

                pipelined(pool, body, 4, STEPS, STEPS, 4)

    def finish(self, tag, half):
        nc, PS = self.nc, self.PS
        L = tag[0]
        base = half * H_TILES
        s = self.norm_sems(tag + "_f")
        (att_copied, aT_done, aT_ready, o_done, o_used, x_ready, xT_done, xT_ready, lg_done, lg_used,
         kept0, kept1) = (
            self.sem(f"{tag}_f_{n}") for n in
            ("att_copied", "aT_done", "aT_ready", "o_done", "o_used", "x_ready", "xT_done", "xT_ready",
             "lg_done", "lg_used", "kept0", "kept1"))
        kept = [kept0, kept1]
        att = self.ring(0, 512, QUAD)
        aT = self.ring(1024, 512)
        xn = self.ring(2048, 512, QUAD)
        xT = self.ring(3072, 512)
        AT_BANK, O_BANK, XT_BANK, LG_BANK = 0, 1, 3, 4

        def stages(t):
            if isinstance(t, int):
                return t < ROUNDS, t >= 1
            return True, True

        with nc.Block() as block:
            @block.gpsimd
            def _(pool):
                def body(i, u):
                    at_least(pool, aT_done, i - 1)
                    pool.tensor_copy(att[u], self.work[:, bass.ds(QUAD * i + base, QUAD), :])\
                        .then_inc(att_copied, 1)

                pipelined(pool, body, 2, ROUNDS, ROUNDS, 2)

            @block.tensor
            def _(pe):
                def body(t, u):
                    one, two = stages(t)
                    if one:
                        pe.wait_ge(att_copied, t + 1)
                        at_least(pe, aT_ready, t)
                        for j in range(QUAD):
                            mm = pe.transpose(PS[:, AT_BANK, j * P:(j + 1) * P], att[u][:, j, :], self.ident)
                        mm.then_inc(aT_done, 1)
                        pe.wait_ge(aT_ready, t + 1)
                        at_least(pe, o_used, t - 1)
                        for j in range(QUAD):
                            mm = pe.matmul(PS[:, O_BANK + u, j * D:(j + 1) * D], aT[u][:, j * P:(j + 1) * P],
                                           self.w_att[f"{L}_o"][:, :], start=True, stop=True)
                        mm.then_inc(o_done, 1)
                    if two:
                        i = t - 1
                        pe.wait_ge(s["xn_done"], QUAD * i + QUAD)
                        at_least(pe, xT_ready, i)
                        for j in range(QUAD):
                            mm = pe.transpose(PS[:, XT_BANK, j * P:(j + 1) * P], xn[1 - u][:, j, :], self.ident)
                        mm.then_inc(xT_done, 1)
                        pe.wait_ge(xT_ready, i + 1)
                        at_least(pe, lg_used, i)
                        for j in range(QUAD):
                            mm = pe.matmul(PS[:, LG_BANK, j * EXPERTS:(j + 1) * EXPERTS],
                                           xT[1 - u][:, j * P:(j + 1) * P], self.w_route[:, :],
                                           start=True, stop=True)
                        mm.then_inc(lg_done, 1)

                pipelined(pe, body, 2, ROUNDS, ROUNDS + 1, 2)

            @block.scalar
            def _(act):
                def body(t, u):
                    one, two = stages(t)
                    if one:
                        act.wait_ge(aT_done, t + 1)
                        act.activation(aT[u], PS[:, AT_BANK, :], ACT.Copy).then_inc(aT_ready, 1)
                    if two:
                        i = t - 1
                        act.wait_ge(xT_done, i + 1)
                        act.activation(xT[1 - u], PS[:, XT_BANK, :], ACT.Copy).then_inc(xT_ready, 1)
                    if one:
                        self.norm_root(act, t, u, s)

                pipelined(act, body, 2, ROUNDS, ROUNDS + 1, 2)

            @block.vector
            def _(dve):
                def body(t, u):
                    one, two = stages(t)
                    if one:
                        X4 = self.X[:, bass.ds(QUAD * t + base, QUAD), :]
                        dve.wait_ge(o_done, t + 1)
                        dve.tensor_tensor(X4, PS[:, O_BANK + u, :].rearrange("p (t d) -> p t d", t=QUAD),
                                          X4, ALU.add).then_inc(o_used, 1)
                        dve.wait_ge(o_used, t + 1)
                        dve.tensor_tensor(X4, X4, self.rows[f"{L}_o"][:, :].unsqueeze(1)
                                          .to_broadcast((P, QUAD, D)), ALU.add).then_inc(x_ready, 1)
                        dve.wait_ge(x_ready, t + 1)
                        self.norm_stats(dve, t, u, s, base)
                    if two:
                        i = t - 1
                        dve.wait_ge(lg_done, i + 1)
                        dve.tensor_tensor(self.logits[:, bass.ds(QUAD * i + base, QUAD), :],
                                          PS[:, LG_BANK, 0:QUAD * EXPERTS].rearrange("p (t e) -> p t e", t=QUAD),
                                          self.b_route[:, :].unsqueeze(1).to_broadcast((P, QUAD, EXPERTS)),
                                          ALU.add).then_inc(lg_used, 1)
                    if one:
                        at_least(dve, kept[u], 8 * (t - u) if not isinstance(t, int) else 16 * (t // 2))
                        self.norm_rows(dve, t, u, s, xn[u], base)

                pipelined(dve, body, 2, ROUNDS, ROUNDS + 1, 2)

            @block.sync
            def _(sp):
                def body(i, u):
                    sp.wait_ge(s["xn_done"], QUAD * i + QUAD)
                    sp.dma_start(self.work[:, bass.ds(QUAD * i + base, QUAD), :], xn[u]).then_inc(kept[u], 16)

                pipelined(sp, body, 2, ROUNDS, ROUNDS, 2)
                for k in kept:
                    sp.wait_ge(k, 16 * (ROUNDS // 2))

    def route(self, tag, half):
        nc, PS = self.nc, self.PS
        done, counted, exp_in, exp_out = (
            self.sem(f"{tag}_r_{n}") for n in ("done", "counted", "exp_in", "exp_out"))
        N = H_TILES * EXPERTS
        big = [self.scratch[:, N * i:N * (i + 1)].rearrange("p (t e) -> p t e", e=EXPERTS)
               for i in range(10)]
        mask1, mask2, picked, tmp, tmp2, total, run0, run1, place, _unused = big
        at = 10 * N
        vec = [self.scratch[:, at + H_TILES * i:at + H_TILES * (i + 1)] for i in range(8)]
        m1, m2, mx, diff, ratio, one_plus, pos, _v = vec
        at += 8 * H_TILES
        eight = [self.scratch[:, at + EXPERTS * i:at + EXPERTS * (i + 1)] for i in range(8)]
        e_cnt, e_a, e_b, e_c, e_base, e_end, e_x, e_y = eight
        at += 8 * EXPERTS
        cmp = self.scratch[:, at:at + SLOT_TILES * EXPERTS].rearrange("p (i e) -> p i e", e=EXPERTS)
        at += SLOT_TILES * EXPERTS
        cnt = self.scratch[:, at:at + SLOT_TILES]
        ints, cols_of = (self.tile_cols[half][:, AHEAD:AHEAD + n] for n in (EXPERTS, SLOT_TILES))
        mine = slice(half * H_TILES, (half + 1) * H_TILES)
        wide = lambda v: v.unsqueeze(2).to_broadcast((P, H_TILES, EXPERTS))
        per_tile = lambda v: v.unsqueeze(1).to_broadcast((P, H_TILES, EXPERTS))
        rank = self.consts[:, C_RANK:C_RANK + EXPERTS]
        starts = self.consts[:, C_START:C_START + SLOT_TILES]

        with nc.Block() as block:
            @block.vector
            def _(dve):
                count = [0]

                def then(ins):
                    count[0] += 1
                    ins.then_inc(done, 1)
                    dve.wait_ge(done, count[0])

                def best(values, best_value, mask):
                    then(dve.tensor_reduce(best_value, values, AX.X, ALU.max))
                    then(dve.tensor_tensor(tmp, values, wide(best_value), ALU.is_equal))
                    then(dve.tensor_tensor(tmp2, tmp, per_tile(rank), ALU.mult))
                    then(dve.tensor_reduce(mx, tmp2, AX.X, ALU.max))
                    then(dve.tensor_tensor(mask, tmp2, wide(mx), ALU.is_equal))

                best(self.logits[:, mine, :], m1, mask1)
                then(dve.scalar_tensor_tensor(out=place, in0=mask1, scalar=-BIG, in1=self.logits[:, mine, :],
                                              op0=ALU.mult, op1=ALU.add))
                best(place, m2, mask2)
                then(dve.tensor_tensor(picked, mask1, mask2, ALU.add))
                dve.tensor_tensor(diff, m2, m1, ALU.subtract).then_inc(exp_in, 1)
                dve.wait_ge(counted, 2)
                then(dve.tensor_copy(total, PS[:, 1, 0:N].rearrange("p (t e) -> p t e", e=EXPERTS)))
                src, dst = total, run0
                k = 1
                while k < H_TILES:
                    then(dve.tensor_copy(dst[:, 0:k, :], src[:, 0:k, :]))
                    then(dve.tensor_tensor(dst[:, k:H_TILES, :], src[:, k:H_TILES, :], src[:, 0:H_TILES - k, :],
                                           ALU.add))
                    src, dst = dst, (run1 if dst is run0 else run0)
                    k *= 2
                then(dve.tensor_scalar(e_cnt, src[:, H_TILES - 1, :], float(P - 1), None, ALU.add))
                then(dve.tensor_copy(ints, e_cnt))
                shift = P.bit_length() - 1
                then(dve.tensor_scalar(ints, ints, shift, shift, ALU.arith_shift_right,
                                       ALU.logical_shift_left))
                then(dve.tensor_copy(e_a, ints))
                cur, nxt, k = e_a, e_b, 1
                while k < EXPERTS:
                    then(dve.tensor_copy(nxt[:, 0:k], cur[:, 0:k]))
                    then(dve.tensor_tensor(nxt[:, k:EXPERTS], cur[:, k:EXPERTS], cur[:, 0:EXPERTS - k],
                                           ALU.add))
                    cur, nxt = nxt, (e_c if nxt is e_b else e_b)
                    k *= 2
                then(dve.tensor_tensor(e_base, cur, e_a, ALU.subtract))
                then(dve.tensor_tensor(place, src, total, ALU.subtract))
                then(dve.tensor_tensor(place, place, per_tile(e_base), ALU.add))
                then(dve.tensor_tensor(place, place, PS[:, 0, 0:N].rearrange("p (t e) -> p t e", e=EXPERTS),
                                       ALU.add))
                for mask, slot in ((mask1, self.slot[0]), (mask2, self.slot[1])):
                    then(dve.tensor_tensor(tmp, place, mask, ALU.mult))
                    then(dve.tensor_reduce(pos, tmp, AX.X, ALU.add))
                    then(dve.tensor_copy(slot[:, mine], pos))
                then(dve.tensor_tensor(cmp, cur.unsqueeze(1).to_broadcast((P, SLOT_TILES, EXPERTS)),
                                       starts.unsqueeze(2).to_broadcast((P, SLOT_TILES, EXPERTS)),
                                       ALU.is_le))
                then(dve.tensor_reduce(cnt, cmp, AX.X, ALU.add))
                then(dve.tensor_scalar(cnt, cnt, float(EXPERTS - 1), float(HIDDEN), ALU.min, ALU.mult))
                then(dve.tensor_copy(cols_of, cnt))
                dve.wait_ge(exp_out, 1)
                then(dve.tensor_scalar(one_plus, ratio, 1.0, None, ALU.add))
                then(dve.reciprocal(self.gate[0][:, mine], one_plus))
                then(dve.tensor_tensor(self.gate[1][:, mine], self.gate[0][:, mine], ratio, ALU.mult))

            @block.tensor
            def _(pe):
                flat = picked.rearrange("p t e -> p (t e)")
                pe.wait_ge(done, 12)
                pe.matmul(PS[:, 0, 0:N], self.tri, flat, start=True, stop=True).then_inc(counted, 1)
                pe.matmul(PS[:, 1, 0:N], self.ones[:, :], flat, start=True, stop=True).then_inc(counted, 1)

            @block.scalar
            def _(act):
                act.wait_ge(exp_in, 1)
                act.activation(ratio, diff, ACT.Exp).then_inc(exp_out, 1)

    def scatter(self, tag, half):
        scattered = self.sem(f"{tag}_scattered")

        def job(pool):
            for t in range(half * H_TILES, (half + 1) * H_TILES):
                for slot in self.slot:
                    pool.indirect_dma_start(
                        self.x_slots[half], bass.IndirectOffsetOnAxis(ap=slot[:, t:t + 1], axis=0),
                        self.work[:, t, :], None).then_inc(scattered, 16)
            pool.wait_ge(scattered, 16 * 2 * H_TILES)
        return job

    def gather(self, tag, half, rows):
        DEEP = 4
        gathered = [self.sem(f"{tag}_g_gathered{i}") for i in range(DEEP)]
        gated, summed = self.sem(f"{tag}_g_gated"), self.sem(f"{tag}_g_summed")
        y = [[rows[:, (2 * i + k) * D:(2 * i + k + 1) * D] for k in range(2)] for i in range(DEEP)]
        first = half * H_TILES

        def job(pool):
            def fetch(n):
                at_least(pool, summed, 2 * (n - DEEP + 1))
                for k in range(2):
                    pool.indirect_dma_start(
                        y[n % DEEP][k], None, self.y_slots[half],
                        bass.IndirectOffsetOnAxis(ap=self.slot[k][:, first + n:first + n + 1], axis=0))\
                        .then_inc(gathered[n % DEEP], 16)

            for n in range(DEEP - 1):
                fetch(n)
            for n in range(H_TILES):
                if n + DEEP - 1 < H_TILES:
                    fetch(n + DEEP - 1)
                t = first + n
                pool.wait_ge(gathered[n % DEEP], 32 * (n // DEEP + 1))
                for k in range(2):
                    pool.tensor_scalar(y[n % DEEP][k], y[n % DEEP][k], self.gate[k][:, t:t + 1], None,
                                       ALU.mult).then_inc(gated, 1)
                for k in range(2):
                    pool.wait_ge(gated, 2 * n + k + 1)
                    at_least(pool, summed, 2 * n + k)
                    pool.tensor_tensor(self.X[:, t, :], self.X[:, t, :], y[n % DEEP][k], ALU.add)\
                        .then_inc(summed, 1)
        return job

    def experts(self, tag, half, pool_job):
        nc, PS = self.nc, self.PS
        (stored0, stored1, xT_done, xT_ready, gate_done, up_done, silu_ready, h_ready,
         hT_done, hT_ready, y_done, y_ready) = (
            self.sem(f"{tag}_e_{n}") for n in
            ("stored0", "stored1", "xT_done", "xT_ready", "gate_done", "up_done",
             "silu_ready", "h_ready", "hT_done", "hT_ready", "y_done", "y_ready"))
        LOADS = 4
        loaded, stored = [self.sem(f"{tag}_e_loaded{i}") for i in range(LOADS)], [stored0, stored1]
        xs = [self.scratch[:, P * i:P * (i + 1)] for i in range(LOADS)]
        xT = [[self.stack[2 * i + k][:, 0:P] for k in range(2)] for i in range(2)]
        w_gate, w_up = self.w_gate, self.w_up
        sg = self.ring(512, 512)
        hid = self.ring(1536, 512)
        hT = self.ring(2560, 512)
        ys = self.ring(3584, 128)
        XT_BANK, GATE_BANK, UP_BANK, HT_BANK, Y_BANK = 0, 1, 3, 5, 7
        N = SLOT_TILES
        LATE = 4
        slot_rows = lambda t: bass.ds(t * P, P)
        x_slots, y_slots = self.x_slots[half], self.y_slots[half]

        def stages(t):
            if isinstance(t, int):
                return t < N, 1 <= t <= N, t >= 2
            return True, True, True

        with nc.Block() as block:
            @block.sync
            def _(sp):
                def body(t, v):
                    if not (isinstance(t, int) and t >= N):
                        at_least(sp, xT_done, t - LOADS + 1)
                        sp.dma_start(xs[v], x_slots[slot_rows(t), :]).then_inc(loaded[v], 16)
                    if not (isinstance(t, int) and t < LATE):
                        i = t - LATE
                        k = (v - LATE) % 2
                        sp.wait_ge(y_ready, i + 1)
                        sp.dma_start(y_slots[slot_rows(i), :], ys[k]).then_inc(stored[k], 16)

                pipelined(sp, body, LATE, N, N + LATE, LOADS)
                for st in stored:
                    sp.wait_ge(st, 16 * (N // 2))

            if pool_job is not None:
                block.gpsimd(pool_job)

            @block.tensor
            def _(pe):
                cols = [None]

                def body(t, v):
                    one, two, three = stages(t)
                    u = v % 2
                    if v == 0:
                        _, cols[0] = nc.values_load_multi_w_load_instructions(
                            self.tile_cols[half][0:1, bass.ds(t, 5)], engines=[nc.tensor.engine],
                            min_val=0, max_val=(EXPERTS - 1) * HIDDEN,
                            skip_runtime_bounds_check_because="route() clamps them")
                    e_new, e_old = cols[0][v + 1], cols[0][v]
                    if one:
                        pe.wait_ge(loaded[v], 4 * (t - v) + 16)
                        at_least(pe, xT_ready, 2 * t)
                        pe.transpose(PS[:, XT_BANK, 0:P], xs[v], self.ident).then_inc(xT_done, 1)
                    if three:
                        i = t - 2
                        pe.wait_ge(h_ready, i + 1)
                        at_least(pe, hT_ready, i - 1)
                        for c in range(CHUNKS):
                            mm = pe.transpose(PS[:, HT_BANK + u, c * P:(c + 1) * P],
                                              hid[u][:, c * P:(c + 1) * P], self.ident)
                        mm.then_inc(hT_done, 1)
                    if two:
                        i = t - 1
                        pe.wait_ge(xT_ready, 2 * i + 2)
                        for w, bank, free, done in ((w_gate, GATE_BANK, silu_ready, gate_done),
                                                    (w_up, UP_BANK, h_ready, up_done)):
                            at_least(pe, free, i - 1)
                            for n, (a, b) in enumerate(((1, 0), (0, 1), (0, 0))):
                                mm = pe.matmul(PS[:, bank + 1 - u, :], xT[1 - u][a],
                                               w[b][:, bass.ds(e_new, HIDDEN)],
                                               start=(n == 0), stop=(n == 2))
                            mm.then_inc(done, 1)
                    if three:
                        pe.wait_ge(hT_ready, t - 1)
                        at_least(pe, y_ready, t - 2)
                        for c in range(CHUNKS):
                            mm = pe.matmul(PS[:, Y_BANK, 0:D], hT[u][:, c * P:(c + 1) * P],
                                           self.w_down[:, bass.ds(e_old + c * D, D)],
                                           start=(c == 0), stop=(c == CHUNKS - 1))
                        mm.then_inc(y_done, 1)

                pipelined(pe, body, 4, N, N + 2, 4)

            @block.scalar
            def _(act):
                def body(t, u):
                    one, two, three = stages(t)
                    if three:
                        i = t - 2
                        act.wait_ge(hT_done, i + 1)
                        act.activation(hT[u], PS[:, HT_BANK + u, :], ACT.Copy).then_inc(hT_ready, 1)
                    if two:
                        i = t - 1
                        act.wait_ge(gate_done, i + 1)
                        act.activation(sg[1 - u], PS[:, GATE_BANK + 1 - u, :], ACT.Silu)\
                           .then_inc(silu_ready, 1)

                pipelined(act, body, 4, N, N + 2, 2)

            @block.vector
            def _(dve):
                def body(t, u):
                    one, two, three = stages(t)
                    if one:
                        dve.wait_ge(xT_done, t + 1)
                        dve.tensor_copy(xT[u][0], PS[:, XT_BANK, 0:P]).then_inc(xT_ready, 1)
                        dve.wait_ge(xT_ready, 2 * t + 1)
                        dve.tensor_tensor(xT[u][1], PS[:, XT_BANK, 0:P], xT[u][0].bitcast(F32),
                                          ALU.subtract).then_inc(xT_ready, 1)
                    if two:
                        i = t - 1
                        dve.wait_ge(silu_ready, i + 1)
                        dve.wait_ge(up_done, i + 1)
                        dve.tensor_tensor(hid[1 - u], PS[:, UP_BANK + 1 - u, :], sg[1 - u], ALU.mult)\
                           .then_inc(h_ready, 1)
                    if three:
                        i = t - 2
                        at_least(dve, stored[u], 8 * (t - u) - 16 if not isinstance(t, int) else 16 * (i // 2))
                        dve.wait_ge(y_done, i + 1)
                        dve.tensor_copy(ys[u], PS[:, Y_BANK, 0:D]).then_inc(y_ready, 1)

                pipelined(dve, body, 4, N, N + 2, 2)

    def combine(self, tag, half):
        nc = self.nc
        DEEP = 8
        gathered = [self.sem(f"{tag}_c_gathered{i}") for i in range(DEEP)]
        half_done, x_done, out_done = (self.sem(f"{tag}_c_{n}") for n in ("half_done", "x_done", "out_done"))
        y = [[self.scratch[:, (2 * i + k) * D:(2 * i + k + 1) * D] for k in range(2)] for i in range(DEEP)]
        first = half * H_TILES
        with nc.Block() as block:
            @block.gpsimd
            def _(pool):
                for n in range(H_TILES):
                    t = first + n
                    at_least(pool, x_done, n - DEEP + 1)
                    for k in range(2):
                        pool.indirect_dma_start(
                            y[n % DEEP][k], None, self.y_slots[half],
                            bass.IndirectOffsetOnAxis(ap=self.slot[k][:, t:t + 1], axis=0))\
                            .then_inc(gathered[n % DEEP], 16)

            @block.vector
            def _(dve):
                for n in range(H_TILES):
                    t = first + n
                    dve.wait_ge(gathered[n % DEEP], 32 * (n // DEEP + 1))
                    for k, step in enumerate((half_done, x_done)):
                        dve.scalar_tensor_tensor(out=self.X[:, t, :], in0=y[n % DEEP][k],
                                                 scalar=self.gate[k][:, t:t + 1], in1=self.X[:, t, :],
                                                 op0=ALU.mult, op1=ALU.add).then_inc(step, 1)
                        if k == 0:
                            dve.wait_ge(half_done, n + 1)

            @block.sync
            def _(sp):
                out = self.dram["out"].rearrange("(t p) d -> p t d", p=P)
                sp.dma_start(out[:, 0:first, :], self.X[:, 0:first, :]).then_inc(out_done, 16)
                for i in range(ROUNDS):
                    sp.wait_ge(x_done, QUAD * (i + 1))
                    t = slice(first + QUAD * i, first + QUAD * (i + 1))
                    sp.dma_start(out[:, t, :], self.X[:, t, :]).then_inc(out_done, 16)
                sp.wait_ge(out_done, 16 * (ROUNDS + 1))


def build(nc, dram):
    with ExitStack() as ctx:
        k = Hybrid(nc, ctx, dram)
        k.setup()
        for layer, causal in (("a", False), ("b", True)):
            for half in range(HALVES):
                tag = f"{layer}{half}"
                job = k.scatter(f"{layer}0", 0) if half == 1 else \
                    (k.gather("a1", 1, k.y_rows) if layer == "b" else None)
                k.project(tag, half, rotary=causal, pool_job=job)
                k.attend(tag + "_s", half, causal)
                k.finish(tag, half)
                k.route(tag, half)
            k.experts(f"{layer}0", 0, k.scatter(f"{layer}1", 1))
            k.experts(f"{layer}1", 1, k.gather(f"{layer}0", 0, k.y_rows))
            if layer == "a":
                k.fresh_semaphores()
        k.combine("b1", 1)


def constants():
    p = np.arange(P)
    keep = np.zeros((P, C_KEEP), np.float32)
    keep[:, C_IDENT:C_IDENT + P] = np.eye(P)
    keep[:, C_TRI:C_TRI + P] = p[:, None] < p[None, :]
    freqs = np.float32(THETA) ** (-np.arange(0, DH, 2, dtype=np.float32) / np.float32(DH))
    angle = np.arange(S, dtype=np.float32)[None, :] * freqs[(p % DH) // 2][:, None]
    keep[:, C_COS:C_COS + S] = np.cos(angle)
    keep[:, C_SIN:C_SIN + S] = np.sin(angle) * np.where(p % 2 == 0, -1, 1)[:, None]
    keep[:, C_KBIAS] = p % ROW == SHIFT_ROW
    keep[:, C_RANK:C_RANK + EXPERTS] = EXPERTS - np.arange(EXPERTS)
    keep[:, C_START:C_START + SLOT_TILES] = np.arange(SLOT_TILES) * P
    staged = np.zeros((P, C_STAGED), np.float32)
    keep[:, C_QMASK + P:C_QMASK + 2 * P] = np.where(p[None, :] > p[:, None], MASKED, 0)
    for a in range(2):
        staged[:, C_KMASK + a * P:C_KMASK + (a + 1) * P] = np.where(p[:, None] > p[None, :], MASKED, 0)
    for n, blocks in enumerate(((0, 1), (2,), (0, 2), (1,))):
        for g in range(GROUPS):
            for j in range(QUAD):
                for b in blocks:
                    for d in range(DH):
                        staged[DH * (QUAD * g + j) + d,
                               C_PERM + (n * GROUPS + g) * P + ROW * j + DH * b + d] = 1
    return keep, staged


def kernel(**inputs):
    import concourse.bacc as _bacc
    from concourse.bass_utils import run_bass_kernel_spmd as _run

    a = {n: np.asarray(v) for n, v in inputs.items()}
    c = np.ascontiguousarray
    keep, staged = constants()
    swap = np.arange(D) ^ 1
    A, Bn, Fn = "L0_attn_a_", "L0_attn_b_", "L0_ffn_"
    arrays = {
        "x": c(a[A + "x"].reshape(TOKENS, D)),
        "consts": keep, "staged": staged,
        "w_a_q": c(a[A + "Wq"].T), "w_a_k": c(a[A + "Wk"].T), "w_a_v": c(a[A + "Wv"].T),
        "w_a_o": c(a[A + "Wff"].T),
        "w_b_q": c(a[Bn + "Wq"].T), "w_b_k": c(a[Bn + "Wk"].T), "w_b_v": c(a[Bn + "Wv"].T),
        "w_b_qs": c(a[Bn + "Wq"][swap].T), "w_b_ks": c(a[Bn + "Wk"][swap].T), "w_b_o": c(a[Bn + "Wo"].T),
        "bias_q": a[Bn + "bq"], "bias_k": a[Bn + "bk"], "bias_qs": c(a[Bn + "bq"][swap]),
        "bias_ks": c(a[Bn + "bk"][swap]), "bias_scale": a[Bn + "scale"],
        "rows_a_o": a[A + "bff"], "rows_b_v": a[Bn + "bv"], "rows_b_o": a[Bn + "bo"],
        "w_route": c(a[Fn + "wg"].T), "b_route": a[Fn + "bg"],
        "w_gate": c(a[Fn + "Wgate"].transpose(2, 0, 1).reshape(D, EXPERTS * HIDDEN)),
        "w_up": c(a[Fn + "Wup"].transpose(2, 0, 1).reshape(D, EXPERTS * HIDDEN)),
        "w_down": c(a[Fn + "Wdown"].reshape(EXPERTS, D, CHUNKS, P).transpose(3, 0, 2, 1)
                    .reshape(P, EXPERTS * CHUNKS * D)),
    }
    from concourse import mybir as _mybir
    nc = _bacc.Bacc("TRN2", target_bir_lowering=False, num_devices=1)
    dram = {n: nc.dram_tensor(f"in_{n}", v.shape, _mybir.dt.from_np(v.dtype), kind="ExternalInput").ap()
            for n, v in arrays.items()}
    dram["out"] = nc.dram_tensor("out", (TOKENS, D), F32, kind="ExternalOutput").ap()
    build(nc, dram)
    r = _run(nc, [{f"in_{n}": v for n, v in arrays.items()}], core_ids=[0])
    return r.results[0]["out"].reshape(B, S, D)
```

```python
from contextlib import ExitStack

import numpy as np
import concourse.bass as bass
from concourse import mybir

F32 = mybir.dt.float32
F32R = mybir.dt.float32r
BF16 = mybir.dt.bfloat16
I32 = mybir.dt.int32
ACT = mybir.ActivationFunctionType
ALU = mybir.AluOpType
AX = mybir.AxisListType

B, S, D = 16, 256, 128
HEADS = 16
DH = D // HEADS
TOKENS = B * S
P = 128
TILES = TOKENS // P
QUAD = 4
GROUPS = HEADS // QUAD
HALVES = 2
H_TOKENS = TOKENS // HALVES
H_TILES = TILES // HALVES
STEPS = B * GROUPS // HALVES
ROUNDS = H_TILES // QUAD
ROW = 32
SHIFT_ROW = 3 * DH
EXPERTS = 8
HIDDEN = 512
CHUNKS = HIDDEN // P
SLOT_TILES = 2 * H_TILES + EXPERTS
EPS = 1e-5
ROUTE_TURNS = (0, 0, 0, 2, 4, 5, 6, 6, 7, 7)
ROUTE_COUNT = 2
WARM_UP = {0: 3, 1: 2, 2: 2, 3: 1, 4: 1, 5: 2, 6: 2}
PICKED = 12
NEWTON = 6
AHEAD = 2
MASKED = -100000.0
THETA = 10000.0
Q_SCALE_A = float(1.0 / np.sqrt(np.float32(D)))
BIG = 3.0e38

C_IDENT = 0
C_TRI = C_IDENT + P
C_COS = C_TRI + P
C_SIN = C_COS + S
C_KBIAS = C_SIN + S
C_RANK = C_KBIAS + 1
C_START = C_RANK + EXPERTS
C_QMASK = C_START + SLOT_TILES
C_KEEP = C_QMASK + 2 * P
N_PERM = 4 * GROUPS * P


def at_least(engine, semaphore, value):
    if not (isinstance(value, int) and value <= 0):
        engine.wait_ge(semaphore, value)


def pipelined(engine, body, first, n, steps, unroll):
    assert first % unroll == 0 and (n - first) % unroll == 0
    for t in range(first):
        body(t, t % unroll)
    with engine.Fori(0, (n - first) // unroll) as turn:
        for u in range(unroll):
            body(turn * unroll + (first + u), u)
    for t in range(n, steps):
        body(t, t % unroll)


class Routing:

    def __init__(self, k, tag, half, bank):
        self.k, self.half = k, half
        (self.done, self.counted, self.exp_in, self.exp_out, self.copied, self.finished) = (
            k.sem(f"{tag}_r_{n}") for n in
            ("done", "counted", "exp_in", "exp_out", "copied", "finished"))
        N = H_TILES * EXPERTS
        room = k.y_rows
        grid = [room[:, N * i:N * (i + 1)].rearrange("p (t e) -> p t e", e=EXPERTS) for i in range(7)]
        self.mask1, self.mask2, self.tmp, self.tmp2, self.picked, self.place, self.before = grid
        self.total = self.picked
        self.flat_picked = room[:, N * 4:N * 5]
        self.counts = [bank[:, N * i:N * (i + 1)].rearrange("p (t e) -> p t e", e=EXPERTS) for i in range(2)]
        self.flat_counts = [bank[:, N * i:N * (i + 1)] for i in range(2)]
        self.cmp = room[:, 2 * N:2 * N + SLOT_TILES * EXPERTS].rearrange("p (i e) -> p i e", e=EXPERTS)
        self.cnt = room[:, 5 * N:5 * N + SLOT_TILES]
        at = 7 * N
        vec = [room[:, at + H_TILES * i:at + H_TILES * (i + 1)] for i in range(7)]
        self.m1, self.m2, self.mx, self.diff, self.ratio, self.one_plus, self.pos = vec
        eight = [k.small[:, EXPERTS * i:EXPERTS * (i + 1)] for i in range(5)]
        self.e_cnt, self.e_a, self.e_b, self.e_c, self.e_base = eight
        self.ints, self.cols_of = (k.tile_cols[half][:, AHEAD:AHEAD + n] for n in (EXPERTS, SLOT_TILES))
        self.mine = slice(half * H_TILES, (half + 1) * H_TILES)
        self.steps = 0
        self.stages = (self.first, self.second, self.pick, self.copy_counts, self.running, self.bases,
                       self.places, self.slots, self.tiles, self.gates)

    def then(self, dve, ins):
        self.steps += 1
        ins.then_inc(self.done, 1)
        dve.wait_ge(self.done, self.steps)

    def wide(self, v):
        return v.unsqueeze(2).to_broadcast((P, H_TILES, EXPERTS))

    def per_tile(self, v):
        return v.unsqueeze(1).to_broadcast((P, H_TILES, EXPERTS))

    def best(self, dve, values, best_value, mask):
        rank = self.k.consts[:, C_RANK:C_RANK + EXPERTS]
        self.then(dve, dve.tensor_reduce(best_value, values, AX.X, ALU.max))
        self.then(dve, dve.tensor_tensor(self.tmp, values, self.wide(best_value), ALU.is_equal))
        self.then(dve, dve.tensor_tensor(self.tmp2, self.tmp, self.per_tile(rank), ALU.mult))
        self.then(dve, dve.tensor_reduce(self.mx, self.tmp2, AX.X, ALU.max))
        self.then(dve, dve.tensor_tensor(mask, self.tmp2, self.wide(self.mx), ALU.is_equal))

    def first(self, dve):
        self.best(dve, self.k.logits[:, self.mine, :], self.m1, self.mask1)
        self.then(dve, dve.scalar_tensor_tensor(out=self.place, in0=self.mask1, scalar=-BIG,
                                                in1=self.k.logits[:, self.mine, :],
                                                op0=ALU.mult, op1=ALU.add))

    def second(self, dve):
        self.best(dve, self.place, self.m2, self.mask2)

    def pick(self, dve):
        self.then(dve, dve.tensor_tensor(self.picked, self.mask1, self.mask2, ALU.add))
        self.picked_at = self.steps
        dve.tensor_tensor(self.diff, self.m2, self.m1, ALU.subtract).then_inc(self.exp_in, 1)

    def count(self, pe):
        pe.wait_ge(self.done, PICKED)
        pe.matmul(self.flat_counts[0], self.k.tri, self.flat_picked, start=True, stop=True)\
          .then_inc(self.counted, 1)
        pe.matmul(self.flat_counts[1], self.k.ones[:, :], self.flat_picked, start=True, stop=True)\
          .then_inc(self.counted, 1)

    def exponential(self, act):
        act.wait_ge(self.exp_in, 1)
        act.activation(self.ratio, self.diff, ACT.Exp).then_inc(self.exp_out, 1)

    def copy_counts(self, dve):
        assert self.picked_at == PICKED
        dve.wait_ge(self.counted, 2)
        dve.tensor_copy(self.before, self.counts[0]).then_inc(self.copied, 1)
        self.then(dve, dve.tensor_copy(self.total, self.counts[1]))

    def running(self, dve):
        dve.wait_ge(self.copied, 1)
        src, dst, k = self.total, self.tmp, 1
        while k < H_TILES:
            self.then(dve, dve.tensor_copy(dst[:, 0:k, :], src[:, 0:k, :]))
            self.then(dve, dve.tensor_tensor(dst[:, k:H_TILES, :], src[:, k:H_TILES, :],
                                             src[:, 0:H_TILES - k, :], ALU.add))
            src, dst = dst, (self.tmp2 if dst is self.tmp else self.tmp)
            k *= 2
        self.run = src

    def bases(self, dve):
        self.then(dve, dve.tensor_scalar(self.e_cnt, self.run[:, H_TILES - 1, :], float(P - 1), None, ALU.add))
        self.then(dve, dve.tensor_copy(self.ints, self.e_cnt))
        shift = P.bit_length() - 1
        self.then(dve, dve.tensor_scalar(self.ints, self.ints, shift, shift, ALU.arith_shift_right,
                                         ALU.logical_shift_left))
        self.then(dve, dve.tensor_copy(self.e_a, self.ints))
        cur, nxt, k = self.e_a, self.e_b, 1
        while k < EXPERTS:
            self.then(dve, dve.tensor_copy(nxt[:, 0:k], cur[:, 0:k]))
            self.then(dve, dve.tensor_tensor(nxt[:, k:EXPERTS], cur[:, k:EXPERTS], cur[:, 0:EXPERTS - k],
                                             ALU.add))
            cur, nxt = nxt, (self.e_c if nxt is self.e_b else self.e_b)
            k *= 2
        self.ends = cur
        self.then(dve, dve.tensor_tensor(self.e_base, cur, self.e_a, ALU.subtract))

    def places(self, dve):
        self.then(dve, dve.tensor_tensor(self.place, self.run, self.total, ALU.subtract))
        self.then(dve, dve.tensor_tensor(self.place, self.place, self.per_tile(self.e_base), ALU.add))
        self.then(dve, dve.tensor_tensor(self.place, self.place, self.before, ALU.add))

    def slots(self, dve):
        for mask, slot in ((self.mask1, self.k.slot[0]), (self.mask2, self.k.slot[1])):
            self.then(dve, dve.tensor_tensor(self.tmp, self.place, mask, ALU.mult))
            self.then(dve, dve.tensor_reduce(self.pos, self.tmp, AX.X, ALU.add))
            self.then(dve, dve.tensor_copy(slot[:, self.mine], self.pos))

    def tiles(self, dve):
        starts = self.k.consts[:, C_START:C_START + SLOT_TILES]
        self.then(dve, dve.tensor_tensor(self.cmp, self.ends.unsqueeze(1).to_broadcast((P, SLOT_TILES, EXPERTS)),
                                         starts.unsqueeze(2).to_broadcast((P, SLOT_TILES, EXPERTS)),
                                         ALU.is_le))
        self.then(dve, dve.tensor_reduce(self.cnt, self.cmp, AX.X, ALU.add))
        self.then(dve, dve.tensor_scalar(self.cnt, self.cnt, float(EXPERTS - 1), float(HIDDEN), ALU.min,
                                         ALU.mult))
        self.then(dve, dve.tensor_copy(self.cols_of, self.cnt))

    def gates(self, dve):
        gate1, gate2 = (g[:, self.mine] for g in self.k.gate)
        dve.wait_ge(self.exp_out, 1)
        self.then(dve, dve.tensor_scalar(self.one_plus, self.ratio, 1.0, None, ALU.add))
        self.then(dve, dve.reciprocal(gate1, self.one_plus))
        dve.tensor_tensor(gate2, gate1, self.ratio, ALU.mult).then_inc(self.finished, 1)


class Hybrid:

    def __init__(self, nc, ctx, dram):
        self.nc, self.ctx, self.dram, self.used = nc, ctx, dram, []
        sb = self.sb
        self.X = sb("X", [P, TILES, D])
        self.work = sb("work", [P, TILES, D])
        self.q_hi = sb("q_hi", [P, H_TOKENS], F32R)
        self.q_lo = sb("q_lo", [P, H_TOKENS], F32R)
        self.k_hi = sb("k_hi", [P, H_TOKENS], F32R)
        self.k_lo = sb("k_lo", [P, H_TOKENS], F32R)
        self.w_gate = [sb(f"w_gate_{n}", [P, EXPERTS * HIDDEN], F32R) for n in ("hi", "lo")]
        self.w_up = [sb(f"w_up_{n}", [P, EXPERTS * HIDDEN], F32R) for n in ("hi", "lo")]
        self.w_down = sb("w_down", [P, EXPERTS * CHUNKS * D])
        self.scratch = sb("scratch", [P, 4096])
        self.consts = sb("consts", [P, C_KEEP])
        self.perm = sb("perm", [P, N_PERM], F32R)
        self.key_mask = sb("key_mask", [P, 2 * P], BF16)
        self.ident_b = sb("ident_b", [P, P], BF16)
        self.ones = sb("ones", [P, P])
        self.eps4 = sb("eps4", [P, 1])
        self.stack = [sb(f"stack{i}", [P, 2 * S], F32R) for i in range(GROUPS)]
        self.q_shifted = [sb(f"q_shifted{i}", [P, S], F32R) for i in range(2)]
        self.row_max = [sb(f"row_max{i}", [P, 2, QUAD, ROW]) for i in range(2)]
        self.v_ones = [sb(f"v_ones{g}", [P, 2, QUAD, ROW]) for g in range(GROUPS)]
        self.out_t = [sb(f"out_t{i}", [P, S]) for i in range(2)]
        self.junk = sb("junk", [P, 2, P + S], BF16)
        self.y_rows = sb("y_rows", [P, 8 * D])
        self.rec_den = sb("rec_den", [P, 2, QUAD])
        self.logits = sb("logits", [P, TILES, EXPERTS])
        self.slot = [sb(f"slot{i}", [P, TILES], I32) for i in range(2)]
        self.gate = [sb(f"gate{i}", [P, TILES]) for i in range(2)]
        self.tile_cols = [sb(f"tile_cols{h}", [P, SLOT_TILES + 2 * AHEAD + 2], I32) for h in range(HALVES)]
        self.stats = [sb(f"stats{i}", [P, QUAD, 6]) for i in range(2)]
        self.mean_var = [sb(f"mean_var{i}", [P, QUAD, 2]) for i in range(ROUNDS)]
        self.root, self.inv, self.inv2, self.rstd, self.norm_shift = (
            [sb(f"{n}{i}", [P, QUAD]) for i in range(ROUNDS)]
            for n in ("root", "inv", "inv_half", "rstd", "norm_shift"))
        self.carrier = sb("carrier", [P, QUAD])
        self.warm = sb("warm", [P, 1])
        self.small = sb("small", [P, 5 * EXPERTS])
        self.w_att = {n: sb(f"w_{n}", [P, D]) for n in
                      ("a_q", "a_k", "a_v", "a_o", "b_q", "b_k", "b_qs", "b_ks", "b_v", "b_o")}
        self.bias = {n: sb(f"bias_{n}", [P, 1]) for n in ("q", "k", "qs", "ks", "scale")}
        self.rows = {n: sb(f"rows_{n}", [P, D]) for n in ("a_o", "b_o")}
        self.v_bias = sb("v_bias", [1, D])
        self.w_route = sb("w_route", [P, EXPERTS])
        self.b_route = sb("b_route", [P, EXPERTS])
        self.PS = ctx.enter_context(nc.psum_tensor("PS", [P, 8, 512], F32))
        self.x_slots, self.y_slots = (
            [nc.dram_tensor(f"{n}_slots{h}", (SLOT_TILES * P, D), F32, kind="Internal").ap()
             for h in range(HALVES)] for n in "xy")
        self.staged_perm = self.work[:, H_TILES:, :].rearrange("p t d -> p (t d)")
        self.staged_mask = self.y_rows[:, 0:2 * P]
        self.ident = self.consts[:, C_IDENT:C_IDENT + P]
        self.tri = self.consts[:, C_TRI:C_TRI + P]
        self.q_mask = self.consts[:, C_QMASK:C_QMASK + 2 * P]

    def sb(self, name, shape, dt=F32):
        return self.ctx.enter_context(self.nc.sbuf_tensor(name, shape, dt))

    def sem(self, name):
        self.used.append(self.nc.alloc_semaphore(name))
        return self.used[-1]

    def fresh_semaphores(self):
        self.nc.clear_and_free_semaphores(self.used)
        self.nc.all_engine_barrier()
        self.used = []

    def setup(self):
        nc, d = self.nc, self.dram
        loaded, small, constant_set = (self.sem(n) for n in ("setup_loaded", "small_loaded", "constant_set"))
        self.x_loaded = [self.sem(f"x_loaded{i}") for i in range(ROUNDS)]
        self.table_loaded = self.sem("table_loaded")
        with nc.Block() as block:
            @block.sync
            def _(sp):
                def load_x(i):
                    tiles = slice(QUAD * i, QUAD * (i + 1))
                    sp.dma_start(self.X[:, tiles, :], self.x_tiles(0)[:, tiles, :]).then_inc(self.x_loaded[i], 16)

                load_x(0)
                sp.dma_start(self.ident, d["consts"][:, C_IDENT:C_IDENT + P]).then_inc(loaded, 16)
                for n in ("a_q", "a_k", "a_v"):
                    sp.dma_start(self.w_att[n][:, :], d[f"w_{n}"]).then_inc(loaded, 16)
                for i in range(1, ROUNDS):
                    load_x(i)
                sp.dma_start(self.consts[:, C_TRI:C_KEEP], d["consts"][:, C_TRI:C_KEEP])\
                  .then_inc(self.table_loaded, 16)
                sp.dma_start(self.staged_perm, d["perm"]).then_inc(self.table_loaded, 16)
                sp.dma_start(self.staged_mask, d["key_mask"]).then_inc(self.table_loaded, 16)
                sp.wait_ge(loaded, 16 * 4)

            @block.scalar
            def _(act):
                act.dma_start(self.rows["a_o"][:, :], self.every_row("rows_a_o", D)).then_inc(small, 16)
                act.wait_ge(small, 16)

            @block.gpsimd
            def _(pool):
                pool.memset(self.ones[:, :], 1.0)
                pool.memset(self.eps4[:, :], EPS / 4)
                for cols in self.tile_cols:
                    pool.memset(cols[:, :], 0)
                for i in range(2):
                    pool.memset(self.row_max[i][:, :, :, :], 0.0)
                for g in range(GROUPS):
                    pool.memset(self.v_ones[g][:, :, :, :], 0.0).then_inc(constant_set, 1)
                    pool.wait_ge(constant_set, g + 1)
                    pool.memset(self.v_ones[g][:, :, :, DH:DH + 1], 1.0)

    def every_row(self, name, n):
        return self.dram[name].rearrange("(o n) -> o n", o=1).to_broadcast((P, n))

    def x_tiles(self, half):
        return self.dram["x"].rearrange("(t p) d -> p t d", p=P)[:, half * H_TILES:(half + 1) * H_TILES, :]

    def tables(self, pool):
        mask_done = self.sem("mask_done")
        pool.wait_ge(self.table_loaded, 16 * 3)
        pool.tensor_copy(self.key_mask[:, :], self.staged_mask).then_inc(mask_done, 1)
        pool.tensor_copy(self.perm[:, :], self.staged_perm)
        pool.tensor_copy(self.ident_b[:, :], self.ident)
        pool.wait_ge(mask_done, 1)
        pool.memset(self.y_rows[:, :], 0.0)

    def weights(self):
        d = self.dram
        piece_loaded = [self.sem(f"piece_loaded{i}") for i in range(2)]
        hi_made, lo_made, rest_loaded, zeroed = (
            self.sem(n) for n in ("weights_hi_made", "weights_lo_made", "rest_loaded", "zeroed"))
        CHUNK, PER_PIECE = EXPERTS * HIDDEN // (STEPS // 2), 4
        COLS = CHUNK * PER_PIECE
        stage = self.work[:, H_TILES:, :].rearrange("p t d -> p (t d)")
        halves = [("w_gate", self.w_gate), ("w_up", self.w_up)]

        def loads(sp):
            n_rest = 0
            sp.dma_start(self.w_att["a_o"][:, :], d["w_a_o"]).then_inc(rest_loaded, 16)
            rest = [(self.w_route[:, :], d["w_route"]), (self.X[:, H_TILES:, :], self.x_tiles(1)),
                    (self.w_down[:, :], d["w_down"])]
            rest += [(self.w_att[n][:, :], d[f"w_{n}"]) for n in self.w_att if n[0] == "b"]
            rest += [(self.bias[n][:, :], d[f"bias_{n}"].rearrange("(p o) -> p o", o=1))
                     for n in ("q", "k", "qs", "ks")]
            rest += [(self.bias["scale"][:, :], self.every_row("bias_scale", 1)),
                     (self.rows["b_o"][:, :], self.every_row("rows_b_o", D)),
                     (self.v_bias[:, :], d["rows_b_v"].rearrange("(o n) -> o n", o=1)),
                     (self.b_route[:, :], self.every_row("b_route", EXPERTS))]
            for p in range(STEPS // PER_PIECE):
                name, _ = halves[p // (STEPS // PER_PIECE // 2)]
                at = p % (STEPS // PER_PIECE // 2) * COLS
                at_least(sp, lo_made, PER_PIECE * (p - 1))
                sp.dma_start(stage[:, p % 2 * COLS:(p % 2 + 1) * COLS], d[name][:, at:at + COLS])\
                  .then_inc(piece_loaded[p % 2], 16)
                if p == 1:
                    for to, src in rest:
                        sp.dma_start(to, src).then_inc(rest_loaded, 16)
                    for h in range(HALVES):
                        rows = self.x_slots[h].rearrange("(p c r) d -> p c (r d)", p=P, r=8)
                        sp.dma_start(rows, self.y_rows[:, :].unsqueeze(1)
                                     .to_broadcast((P, SLOT_TILES // 8, 8 * D))).then_inc(zeroed, 16)
            sp.wait_ge(rest_loaded, 16 * (1 + len(rest)))
            sp.wait_ge(zeroed, 16 * HALVES)

        def split(pool, s):
            p = s // PER_PIECE
            _, (hi, lo) = halves[s // (STEPS // 2)]
            at = s % (STEPS // 2) * CHUNK
            to = slice(at, at + CHUNK)
            raw = stage[:, p % 2 * COLS + s % PER_PIECE * CHUNK:p % 2 * COLS + (s % PER_PIECE + 1) * CHUNK]
            pool.wait_ge(piece_loaded[p % 2], 16 * (p // 2 + 1))
            pool.tensor_copy(hi[:, to], raw).then_inc(hi_made, 1)
            pool.wait_ge(hi_made, s + 1)
            pool.tensor_tensor(lo[:, to], raw, hi[:, to].bitcast(F32), ALU.subtract).then_inc(lo_made, 1)

        return loads, split

    def norm_sems(self, tag):
        return {n: self.sem(f"{tag}_{n}") for n in
                ("stats_done", "var_done", "root_done", "newton_done", "xn_act_done", "xn_dve_done")}

    def carry_wait(self, dve, j=0):
        dve.memset(self.carrier[:, j:j + 1], 0.0)

    def norm_stats(self, dve, i, s, base):
        for j in range(QUAD):
            dve.bn_stats(self.stats[i % 2][:, j, :], self.X[:, base + QUAD * i + j, :])\
               .then_inc(s["stats_done"], 1)
        dve.wait_ge(s["stats_done"], QUAD * i + QUAD)
        for j in range(QUAD):
            dve.bn_aggr(self.mean_var[i][:, j, :], self.stats[i % 2][:, j, :]).then_inc(s["var_done"], 1)

    def norm_root(self, act, i, s):
        act.wait_ge(s["var_done"], QUAD * i + QUAD)
        act.activation(self.root[i][:, :], self.mean_var[i][:, :, 1], ACT.Sqrt,
                       bias=self.eps4[:, :], scale=0.25).then_inc(s["root_done"], 1)

    def norm_newton(self, dve, i, s):
        dve.wait_ge(s["root_done"], i + 1)
        step = s["newton_done"]
        dve.reciprocal(self.inv[i][:, :], self.root[i][:, :]).then_inc(step, 1)
        dve.tensor_scalar(self.inv2[i][:, :], self.mean_var[i][:, :, 1], EPS, 0.25, ALU.add,
                          ALU.mult).then_inc(step, 1)
        dve.wait_ge(step, NEWTON * i + 2)
        dve.tensor_tensor(self.inv2[i][:, :], self.inv2[i][:, :], self.inv[i][:, :], ALU.mult).then_inc(step, 1)
        dve.wait_ge(step, NEWTON * i + 3)
        dve.tensor_tensor(self.inv[i][:, :], self.inv2[i][:, :], self.root[i][:, :], ALU.add).then_inc(step, 1)
        dve.wait_ge(step, NEWTON * i + 4)
        dve.reciprocal(self.rstd[i][:, :], self.inv[i][:, :]).then_inc(step, 1)
        dve.wait_ge(step, NEWTON * i + 5)
        dve.scalar_tensor_tensor(out=self.norm_shift[i][:, :], in0=self.mean_var[i][:, :, 0], scalar=-1.0,
                                 in1=self.rstd[i][:, :], op0=ALU.mult, op1=ALU.mult).then_inc(step, 1)

    def norm_rows(self, act, i, s, xn, base):
        act.wait_ge(s["newton_done"], NEWTON * (i + 1))
        for j in range(0, QUAD // 2):
            act.activation(xn[:, j, :], self.X[:, base + QUAD * i + j, :], ACT.Identity,
                           bias=self.norm_shift[i][:, j:j + 1], scale=self.rstd[i][:, j:j + 1])\
               .then_inc(s["xn_act_done"], 1)

    def norm_rows_dve(self, dve, i, s, xn, base):
        for j in range(QUAD // 2, QUAD):
            dve.tensor_scalar(xn[:, j, :], self.X[:, base + QUAD * i + j, :], self.mean_var[i][:, j, 0:1],
                              self.rstd[i][:, j:j + 1], ALU.subtract, ALU.mult).then_inc(s["xn_dve_done"], 1)

    def wait_rows(self, pe, i, s):
        for name in ("xn_act_done", "xn_dve_done"):
            pe.wait_ge(s[name], QUAD // 2 * (i + 1))

    def ring(self, at, n, *dims):
        out = []
        for i in range(2):
            v = self.scratch[:, at + i * n:at + (i + 1) * n]
            if dims:
                v = v.rearrange("p (t d) -> p t d", t=dims[0])
            out.append(v)
        return out

    def rows_product(self, pe, out, xT, weights, bias):
        for j in range(QUAD):
            at = out[:, j * D:(j + 1) * D]
            mm = pe.matmul(at, xT[:, j * P:(j + 1) * P], weights[:, :], start=True, stop=bias is None)
            if bias is not None:
                mm = pe.matmul(at, self.ones[0:1, :], bias[:, :], start=False, stop=True)
        return mm

    def project(self, tag, half, rotary, pool_job=None):
        nc, PS = self.nc, self.PS
        base = half * H_TILES
        s = self.norm_sems(tag)
        xT_done, xT_ready, proj_done, v_done, hi_ready, rot_done, qk_used, v_used, warm = (
            self.sem(f"{tag}_{n}") for n in ("xT_done", "xT_ready", "proj_done", "v_done", "hi_ready",
                                             "rot_done", "qk_used", "v_used", "warm"))
        xn = self.ring(0, 512, QUAD)
        xT = self.ring(1024, 512)
        turned = [self.scratch[:, 2048 + 512 * i:2560 + 512 * i] for i in range(2)]
        part = [self.scratch[:, 3072 + 512 * i:3584 + 512 * i] for i in range(2)]
        kinds = ("q", "qs", "k", "ks") if rotary else ("q", "k")
        L = "b" if rotary else "a"
        T_BANK, V_BANK = 0, 7
        bank = {"q": 1, "k": 2, "qs": 3, "ks": 4}
        hi = {"q": self.q_hi, "k": self.k_hi}
        lo = {"q": self.q_lo, "k": self.k_lo}
        cols = lambda i: slice(i * 512, (i + 1) * 512)
        ROT = 3

        with nc.Block() as block:
            if pool_job is not None:
                block.gpsimd(pool_job)

            @block.vector
            def _(dve):
                def rotate(i, n):
                    kind = "qk"[n]
                    at_least(dve, rot_done, 2 * ROT * i + ROT * n)
                    for m, (src, trig) in enumerate(((kind, C_COS), (kind + "s", C_SIN))):
                        dve.wait_ge(proj_done, len(kinds) * i + kinds.index(src) + 1)
                        dve.scalar_tensor_tensor(
                            out=part[m].rearrange("p (b s) -> p b s", b=2),
                            in0=PS[:, bank[src], :].rearrange("p (b s) -> p b s", b=2),
                            scalar=self.bias[src][:, 0:1],
                            in1=self.consts[:, trig:trig + S].unsqueeze(1).to_broadcast((P, 2, S)),
                            op0=ALU.add, op1=ALU.mult).then_inc(rot_done, 1)
                    dve.wait_ge(rot_done, 2 * ROT * i + ROT * n + 2)
                    at_least(dve, qk_used, 2 * i + n - 1)
                    dve.tensor_tensor(turned[n], part[0], part[1], ALU.add).then_inc(rot_done, 1)

                def low_part(i, n):
                    kind = "qk"[n]
                    dve.wait_ge(hi_ready, 2 * i + n + 1)
                    value = turned[n] if rotary else PS[:, bank[kind], :]
                    scale = (self.bias["scale"][:, 0:1] if rotary else Q_SCALE_A) if kind == "q" else 1.0
                    dve.scalar_tensor_tensor(out=lo[kind][:, cols(i)], in0=value, scalar=scale,
                                             in1=hi[kind][:, cols(i)].bitcast(F32), op0=ALU.mult,
                                             op1=ALU.subtract).then_inc(qk_used, 1)

                for t in range(ROUNDS + 1):
                    if t < ROUNDS:
                        if tag == "a0":
                            dve.wait_ge(self.x_loaded[t], 16)
                        self.norm_stats(dve, t, s, base)
                    if rotary and t >= 1:
                        rotate(t - 1, 0)
                    if t < ROUNDS:
                        self.norm_newton(dve, t, s)
                        at_least(dve, xT_done, t - 1)
                        self.norm_rows_dve(dve, t, s, xn[t % 2], base)
                    if rotary and t >= 1:
                        rotate(t - 1, 1)
                    if t >= 1:
                        low_part(t - 1, 0)
                        low_part(t - 1, 1)

            @block.tensor
            def _(pe):
                for i in range(ROUNDS):
                    self.wait_rows(pe, i, s)
                    at_least(pe, xT_ready, i)
                    for j in range(QUAD):
                        mm = pe.transpose(PS[:, T_BANK, j * P:(j + 1) * P], xn[i % 2][:, j, :], self.ident)
                    mm.then_inc(xT_done, 1)
                    pe.wait_ge(xT_ready, i + 1)
                    for kind in kinds:
                        n = "qk".index(kind[0])
                        if rotary:
                            at_least(pe, rot_done, 2 * ROT * (i - 1) + ROT * n + (1 if kind == "qk"[n] else 2)
                                     if i else 0)
                        else:
                            at_least(pe, qk_used, 2 * (i - 1) + n + 1 if i else 0)
                        pe.matmul(PS[:, bank[kind], :], self.w_att[f"{L}_{kind}"][:, :], xT[i % 2],
                                  start=True, stop=True).then_inc(proj_done, 1)
                    at_least(pe, v_used, i)
                    self.rows_product(pe, PS[:, V_BANK, :], xT[i % 2], self.w_att[f"{L}_v"],
                                      self.v_bias if rotary else None).then_inc(v_done, 1)

            @block.scalar
            def _(act):
                def high_part(i, n):
                    kind = "qk"[n]
                    if rotary:
                        act.wait_ge(rot_done, 2 * ROT * i + ROT * n + ROT)
                    else:
                        act.wait_ge(proj_done, 2 * i + n + 1)
                    value = turned[n] if rotary else PS[:, bank[kind], :]
                    scale = (self.bias["scale"][:, 0:1] if rotary else Q_SCALE_A) if kind == "q" else 1.0
                    act.activation(hi[kind][:, cols(i)], value, ACT.Copy, scale=scale).then_inc(hi_ready, 1)

                act.activation(self.warm[:, :], self.eps4[:, :], ACT.Sqrt).then_inc(warm, 1)
                for t in range(ROUNDS + 1):
                    if t < ROUNDS:
                        self.norm_root(act, t, s)
                    if t >= 1:
                        high_part(t - 1, 0)
                    if t < ROUNDS:
                        at_least(act, xT_done, t - 1)
                        self.norm_rows(act, t, s, xn[t % 2], base)
                        act.wait_ge(xT_done, t + 1)
                        at_least(act, v_done, t - 1)
                        act.activation(xT[t % 2], PS[:, T_BANK, :], ACT.Copy).then_inc(xT_ready, 1)
                    if t >= 1:
                        high_part(t - 1, 1)
                        i = t - 1
                        act.wait_ge(v_done, i + 1)
                        act.activation(self.work[:, base + QUAD * i:base + QUAD * (i + 1), :],
                                       PS[:, V_BANK, :].rearrange("p (t d) -> p t d", t=QUAD),
                                       ACT.Copy).then_inc(v_used, 1)

    def attend(self, tag, half, causal, between=None, loads=None, routing=None):
        nc, PS = self.nc, self.PS
        base = half * H_TILES
        (stack_done, stack_ready, score_done, max_ready, shift_done, q_ready, scoreT_done, probs_ready,
         pv_done, outT_ready, out_done, rec_ready, out_used, v_ready) = (
            self.sem(f"{tag}_{n}") for n in
            ("stack_done", "stack_ready", "score_done", "max_ready", "shift_done", "q_ready",
             "scoreT_done", "probs_ready", "pv_done", "outT_ready", "out_done", "rec_ready",
             "out_used", "v_ready"))
        probs = [self.scratch[:, 2048 * i:2048 * (i + 1)].rearrange("p (j n) -> p j n", j=QUAD)
                 for i in range(2)]
        KEYS_BANK, SCORE_BANK, PV_BANK, STACK_BANK = 0, 4, 6, 7
        per_head = 2 if causal else 1
        left = P if causal else 0

        def exists(t, late):
            return not isinstance(t, int) or 0 <= t - late < STEPS

        with nc.Block() as block:
            @block.tensor
            def _(pe):
                def stack_parts(t, g):
                    at_least(pe, stack_ready, 2 * t)
                    at_least(pe, q_ready, t - 1)
                    tokens = bass.ds((t - g) * (S // GROUPS), S)
                    for n, parts in enumerate(((self.q_hi, self.q_lo), (self.k_hi, self.k_lo))):
                        for m, part in enumerate(parts):
                            c = ((2 * n + m) * GROUPS + g) * P
                            mm = pe.matmul(PS[:, STACK_BANK, n * S:(n + 1) * S], self.perm[:, c:c + P],
                                           part[:, tokens], start=(m == 0), stop=(m == 1))
                    mm.then_inc(stack_done, 1)

                def scores(s, g, j):
                    at_least(pe, max_ready, per_head * (QUAD * s + j - 1))
                    out = PS[:, SCORE_BANK + j % 2, :]
                    if isinstance(s, int) and s in WARM_UP:
                        for _ in range(WARM_UP[s]):
                            pe.matmul(out, self.perm[:, 0:P], self.perm[:, 0:2 * S], start=True, stop=True)
                    r = slice(ROW * j, ROW * j + ROW)
                    for q in range(2):
                        mm = pe.matmul(out[:, q * S:(q + 1) * S], self.stack[g][r, q * P:(q + 1) * P],
                                       self.stack[g][r, S:2 * S], start=True, stop=True,
                                       skip_group_check=True)
                    mm.then_inc(score_done, 1)

                def shifts(s, g):
                    pe.wait_ge(max_ready, per_head * QUAD * (s + 1))
                    for q in range(2):
                        mm = pe.transpose(PS[:, STACK_BANK, q * P:(q + 1) * P],
                                          self.row_max[g % 2][:, q, :, :].rearrange("p j r -> p (j r)"),
                                          self.ident)
                    mm.then_inc(shift_done, 1)

                def scores_t(s, g, part):
                    at_least(pe, probs_ready, 2 * s + part - 1)
                    for j in (2 * part, 2 * part + 1):
                        out = PS[:, KEYS_BANK + j, :]
                        r = slice(ROW * j, ROW * j + ROW)
                        for k in range(2):
                            at = (1 - k) * S
                            mm = pe.matmul(out[:, at:at + S], self.stack[g][r, S + k * P:S + (k + 1) * P],
                                           self.q_shifted[g % 2][r, :], start=(k == 0),
                                           stop=(k == 1 and not causal), skip_group_check=True)
                        if causal:
                            mm = pe.matmul(out[:, P:3 * P], self.ident_b[:, :], self.key_mask[:, :],
                                           start=False, stop=True, skip_group_check=True)
                    mm.then_inc(scoreT_done, 1)

                def products(s, g):
                    for k in range(2):
                        skip = left if k == 1 else 0
                        at = (1 - k) * S + skip
                        for j in range(QUAD):
                            mm = pe.matmul(PS[ROW * j:ROW * j + ROW, PV_BANK, skip:S],
                                           self.v_ones[g][:, k, j, :], probs[g % 2][:, j, at:at + S - skip],
                                           start=(k == 0), stop=(k == 1), skip_group_check=True)
                    mm.then_inc(pv_done, 1)

                def body(t, g):
                    if routing is not None and isinstance(t, int) and t == ROUTE_COUNT:
                        routing.count(pe)
                    if routing is not None and isinstance(t, int) and t == 4:
                        pe.wait_ge(routing.done, PICKED + 1)
                        pe.wait_ge(routing.copied, 1)
                    g1, g2, g3 = ((g - late) % GROUPS for late in (1, 2, 3))
                    if exists(t, 1):
                        pe.wait_ge(stack_ready, 2 * t)
                        scores(t - 1, g1, 0)
                    if exists(t, 2):
                        shifts(t - 2, g2)
                    if exists(t, 3):
                        pe.wait_ge(q_ready, t - 2)
                        scores_t(t - 3, g3, 0)
                    if exists(t, 1):
                        scores(t - 1, g1, 1)
                    if exists(t, 5):
                        pe.wait_ge(outT_ready, t - 4)
                        for q in range(2):
                            mm = pe.transpose(PS[:, PV_BANK, S + q * P:S + (q + 1) * P],
                                              self.out_t[g1 % 2][:, q * P:(q + 1) * P], self.ident)
                        mm.then_inc(out_done, 1)
                    if exists(t, 3):
                        scores_t(t - 3, g3, 1)
                    if exists(t, 1):
                        scores(t - 1, g1, 2)
                    if exists(t, 0):
                        stack_parts(t, g)
                    if exists(t, 1):
                        scores(t - 1, g1, 3)
                    if exists(t, 4):
                        pe.wait_ge(probs_ready, 2 * (t - 3))
                        pe.wait_ge(v_ready, t - 3)
                        at_least(pe, out_used, t - 4)
                        products(t - 4, g)

                pipelined(pe, body, 8, STEPS, STEPS + 5, 4)

            @block.scalar
            def _(act):
                def body(t, g):
                    if routing is not None and isinstance(t, int) and t == ROUTE_COUNT:
                        routing.exponential(act)
                    if exists(t, 5):
                        act.wait_ge(pv_done, t - 4)
                        at_least(act, out_done, t - 6)
                        act.activation(self.out_t[(g - 1) % 2][:, :], PS[:, PV_BANK, 0:S], ACT.Copy)\
                           .then_inc(outT_ready, 1)
                    if exists(t, 3):
                        s = t - 3
                        for part in range(2):
                            act.wait_ge(scoreT_done, 2 * s + part + 1)
                            at_least(act, pv_done, s - 1)
                            act.activation(probs[(g - 3) % 2][:, 2 * part:2 * part + 2, left:2 * S],
                                           PS[:, KEYS_BANK + 2 * part:KEYS_BANK + 2 * part + 2, left:2 * S],
                                           ACT.Exp).then_inc(probs_ready, 1)
                    if exists(t, 0):
                        act.wait_ge(stack_done, t + 1)
                        at_least(act, scoreT_done, 2 * (t - 3))
                        act.activation(self.stack[g][:, 0:S], PS[:, STACK_BANK, 0:S], ACT.Copy)\
                           .then_inc(stack_ready, 1)
                        act.activation(self.stack[g][:, S:2 * S], PS[:, STACK_BANK, S:2 * S], ACT.Identity,
                                       bias=self.consts[:, C_KBIAS:C_KBIAS + 1]).then_inc(stack_ready, 1)

                pipelined(act, body, 8, STEPS, STEPS + 5, 4)

            @block.vector
            def _(dve):
                def maxima(s, g, j):
                    dve.wait_ge(score_done, QUAD * s + j + 1)
                    out = PS[:, SCORE_BANK + j % 2, :]
                    to = self.row_max[g % 2]
                    if not causal:
                        dve.tensor_reduce(to[:, :, j, SHIFT_ROW:SHIFT_ROW + 1],
                                          out.rearrange("p (q k) -> p q k", q=2),
                                          AX.X, ALU.max).then_inc(max_ready, 1)
                        return
                    self.carry_wait(dve, j)
                    junk = self.junk[:, j % 2, :]
                    dve.tensor_tensor_reduce(junk[:, 0:P], out[:, 0:P], self.q_mask[:, P:2 * P], 1.0, -BIG,
                                             ALU.add, ALU.max, to[:, 0, j, SHIFT_ROW:SHIFT_ROW + 1])\
                       .then_inc(max_ready, 1)
                    dve.tensor_tensor_reduce(junk[:, P:P + S], out[:, S:2 * S], self.q_mask, 1.0, -BIG, ALU.add,
                                             ALU.max, to[:, 1, j, SHIFT_ROW:SHIFT_ROW + 1])\
                       .then_inc(max_ready, 1)

                def body(t, g):
                    g1, g2 = ((g - late) % GROUPS for late in (1, 2))
                    if exists(t, 1):
                        maxima(t - 1, g1, 0)
                    if exists(t, 2):
                        dve.wait_ge(shift_done, t - 1)
                        dve.tensor_tensor(self.q_shifted[g % 2][:, :], self.stack[g2][:, 0:S].bitcast(F32),
                                          PS[:, STACK_BANK, 0:S], ALU.subtract).then_inc(q_ready, 1)
                    if exists(t, 1):
                        maxima(t - 1, g1, 1)
                    if exists(t, 5):
                        s = t - 5
                        dve.wait_ge(out_done, s + 1)
                        rows = PS[:, PV_BANK, S:2 * S].rearrange("p (q j r) -> p q j r", q=2, j=QUAD)
                        dve.reciprocal(self.rec_den[:, :, :], rows[:, :, :, DH]).then_inc(rec_ready, 1)
                        dve.wait_ge(rec_ready, s + 1)
                        batch2 = (s - g1) // 2 if isinstance(s, int) else (t - (g1 + 5)) // 2
                        out = self.work[:, bass.ds(batch2 + base, 2), ROW * g1:ROW * g1 + ROW]\
                            .rearrange("p q (j d) -> p q j d", j=QUAD)
                        dve.tensor_tensor(out, rows[:, :, :, 0:DH],
                                          self.rec_den[:, :, :].unsqueeze(3).to_broadcast((P, 2, QUAD, DH)),
                                          ALU.mult).then_inc(out_used, 1)
                    if exists(t, 1):
                        maxima(t - 1, g1, 2)
                        maxima(t - 1, g1, 3)
                    if routing is not None and isinstance(t, int):
                        for n, turn in enumerate(ROUTE_TURNS):
                            if t == turn:
                                routing.stages[n](dve)

                pipelined(dve, body, 8, STEPS, STEPS + 5, 4)

            if loads is not None:
                block.sync(loads)

            @block.gpsimd
            def _(pool):
                def body(s, g):
                    at_least(pool, pv_done, s - 3)
                    tiles = bass.ds((s - g) // 2 + base, 2)
                    pool.tensor_copy(self.v_ones[g][:, :, :, 0:DH],
                                     self.work[:, tiles, ROW * g:ROW * g + ROW]
                                     .rearrange("p q (j d) -> p q j d", j=QUAD)).then_inc(v_ready, 1)
                    if g == GROUPS - 1:
                        pool.tensor_tensor(self.X[:, tiles, :], self.X[:, tiles, :],
                                           self.rows[tag[0] + "_o"][:, :].unsqueeze(1)
                                           .to_broadcast((P, 2, D)), ALU.add)

                if between is None:
                    pipelined(pool, body, 4, STEPS, STEPS, 4)
                else:
                    for s in range(STEPS):
                        body(s, s % GROUPS)
                        between(pool, s)

    def finish(self, tag, half):
        nc, PS = self.nc, self.PS
        L = tag[0]
        base = half * H_TILES
        s = self.norm_sems(tag + "_f")
        (aT_done, aT_ready, o_done, x_ready, xT_done, xT_ready, lg_done, lg_used, warm) = (
            self.sem(f"{tag}_f_{n}") for n in
            ("aT_done", "aT_ready", "o_done", "x_ready", "xT_done", "xT_ready", "lg_done", "lg_used", "warm"))
        aT = self.ring(0, 512)
        xT = self.ring(1024, 512)
        AT_BANK, O_BANK, XT_BANK, LG_BANK = 0, 2, 4, 6
        tiles = lambda i: slice(base + QUAD * i, base + QUAD * (i + 1))

        with nc.Block() as block:
            @block.tensor
            def _(pe):
                def transposed(bank, rows, done):
                    for j in range(QUAD):
                        mm = pe.transpose(PS[:, bank, j * P:(j + 1) * P], rows[:, j, :], self.ident)
                    mm.then_inc(done, 1)

                for t in range(ROUNDS + 2):
                    if t < ROUNDS:
                        at_least(pe, aT_ready, t - 1)
                        transposed(AT_BANK + t % 2, self.work[:, tiles(t), :], aT_done)
                    if 1 <= t <= ROUNDS:
                        i = t - 1
                        pe.wait_ge(aT_ready, i + 1)
                        at_least(pe, x_ready, i - 1)
                        self.rows_product(pe, PS[:, O_BANK + i % 2, :], aT[i % 2], self.w_att[f"{L}_o"],
                                          None).then_inc(o_done, 1)
                    if t >= 2:
                        i = t - 2
                        self.wait_rows(pe, i, s)
                        at_least(pe, xT_ready, i - 1)
                        transposed(XT_BANK + i % 2, self.work[:, tiles(i), :], xT_done)
                        pe.wait_ge(xT_ready, i + 1)
                        at_least(pe, lg_used, i - 1)
                        for j in range(QUAD):
                            mm = pe.matmul(PS[:, LG_BANK + i % 2, j * EXPERTS:(j + 1) * EXPERTS],
                                           xT[i % 2][:, j * P:(j + 1) * P], self.w_route[:, :],
                                           start=True, stop=True)
                        mm.then_inc(lg_done, 1)

            @block.scalar
            def _(act):
                act.activation(self.warm[:, :], self.eps4[:, :], ACT.Sqrt).then_inc(warm, 1)
                for t in range(ROUNDS + 2):
                    if t < ROUNDS:
                        act.wait_ge(aT_done, t + 1)
                        at_least(act, o_done, t - 1)
                        act.activation(aT[t % 2], PS[:, AT_BANK + t % 2, :], ACT.Copy).then_inc(aT_ready, 1)
                    if t >= 2:
                        i = t - 2
                        act.wait_ge(xT_done, i + 1)
                        at_least(act, lg_done, i - 1)
                        act.activation(xT[i % 2], PS[:, XT_BANK + i % 2, :], ACT.Copy).then_inc(xT_ready, 1)
                    if 1 <= t <= ROUNDS:
                        self.norm_root(act, t - 1, s)
                        self.norm_rows(act, t - 1, s, self.work[:, tiles(t - 1), :], base)

            @block.vector
            def _(dve):
                for t in range(1, ROUNDS + 2):
                    if t <= ROUNDS:
                        i = t - 1
                        X4 = self.X[:, tiles(i), :]
                        dve.wait_ge(o_done, i + 1)
                        dve.tensor_tensor(X4, PS[:, O_BANK + i % 2, :].rearrange("p (t d) -> p t d", t=QUAD),
                                          X4, ALU.add).then_inc(x_ready, 1)
                        dve.wait_ge(x_ready, i + 1)
                        self.norm_stats(dve, i, s, base)
                    if t <= ROUNDS:
                        self.norm_newton(dve, t - 1, s)
                        self.norm_rows_dve(dve, t - 1, s, self.work[:, tiles(t - 1), :], base)
                    if t >= 2:
                        i = t - 2
                        dve.wait_ge(lg_done, i + 1)
                        dve.tensor_tensor(self.logits[:, tiles(i), :],
                                          PS[:, LG_BANK + i % 2, 0:QUAD * EXPERTS]
                                          .rearrange("p (t e) -> p t e", t=QUAD),
                                          self.b_route[:, :].unsqueeze(1).to_broadcast((P, QUAD, EXPERTS)),
                                          ALU.add).then_inc(lg_used, 1)

    def scatter(self, tag, half, routing=None):
        scattered = self.sem(f"{tag}_scattered")

        def step(pool, n):
            if n == 0 and routing is not None:
                pool.wait_ge(routing.finished, 1)
            t = half * H_TILES + n
            for slot in self.slot:
                pool.indirect_dma_start(
                    self.x_slots[half], bass.IndirectOffsetOnAxis(ap=slot[:, t:t + 1], axis=0),
                    self.work[:, t, :], None).then_inc(scattered, 16)
            if n == H_TILES - 1:
                pool.wait_ge(scattered, 16 * 2 * H_TILES)
        return step

    def gather(self, tag, half, rows):
        DEEP = 4
        gathered = [self.sem(f"{tag}_g_gathered{i}") for i in range(DEEP)]
        gated, summed = self.sem(f"{tag}_g_gated"), self.sem(f"{tag}_g_summed")
        y = [[rows[:, (2 * i + k) * D:(2 * i + k + 1) * D] for k in range(2)] for i in range(DEEP)]
        first = half * H_TILES

        def fetch(pool, n):
            at_least(pool, summed, 2 * (n - DEEP + 1))
            for k in range(2):
                pool.indirect_dma_start(
                    y[n % DEEP][k], None, self.y_slots[half],
                    bass.IndirectOffsetOnAxis(ap=self.slot[k][:, first + n:first + n + 1], axis=0))\
                    .then_inc(gathered[n % DEEP], 16)

        def step(pool, n):
            for ahead in range(DEEP - 1 if n else 0, DEEP):
                if n + ahead < H_TILES:
                    fetch(pool, n + ahead)
            t = first + n
            pool.wait_ge(gathered[n % DEEP], 32 * (n // DEEP + 1))
            for k in range(2):
                pool.tensor_scalar(y[n % DEEP][k], y[n % DEEP][k], self.gate[k][:, t:t + 1], None,
                                   ALU.mult).then_inc(gated, 1)
            for k in range(2):
                pool.wait_ge(gated, 2 * n + k + 1)
                at_least(pool, summed, 2 * n + k)
                pool.tensor_tensor(self.X[:, t, :], self.X[:, t, :], y[n % DEEP][k], ALU.add)\
                    .then_inc(summed, 1)
        return step

    def experts(self, tag, half, pool_job, routing=None):
        nc, PS = self.nc, self.PS
        (stored0, stored1, xT_done, xT_ready, gate_done, up_done, silu_ready, h_ready,
         hT_done, hT_ready, y_done, y_ready) = (
            self.sem(f"{tag}_e_{n}") for n in
            ("stored0", "stored1", "xT_done", "xT_ready", "gate_done", "up_done",
             "silu_ready", "h_ready", "hT_done", "hT_ready", "y_done", "y_ready"))
        LOADS = 4
        loaded, stored = [self.sem(f"{tag}_e_loaded{i}") for i in range(LOADS)], [stored0, stored1]
        xs = [self.scratch[:, P * i:P * (i + 1)] for i in range(LOADS)]
        xT = [[self.stack[2 * i + k][:, 0:P] for k in range(2)] for i in range(2)]
        w_gate, w_up = self.w_gate, self.w_up
        sg = self.ring(512, 512)
        hid = self.ring(1536, 512)
        hT = self.ring(2560, 512)
        ys = self.ring(3584, 128)
        XT_BANK, GATE_BANK, UP_BANK, HT_BANK, Y_BANK = 0, 1, 3, 5, 7
        BEFORE = 4
        N = SLOT_TILES
        LATE = 4
        slot_rows = lambda t: bass.ds(t * P, P)
        x_slots, y_slots = self.x_slots[half], self.y_slots[half]

        def stages(t):
            if isinstance(t, int):
                return t < N, 1 <= t <= N, t >= 2
            return True, True, True

        with nc.Block() as block:
            @block.sync
            def _(sp):
                def body(t, v):
                    if not (isinstance(t, int) and t >= N):
                        at_least(sp, xT_done, t - LOADS + 1)
                        sp.dma_start(xs[v], x_slots[slot_rows(t), :]).then_inc(loaded[v], 16)
                    if not (isinstance(t, int) and t < LATE):
                        i = t - LATE
                        k = (v - LATE) % 2
                        sp.wait_ge(y_ready, i + 1)
                        sp.dma_start(y_slots[slot_rows(i), :], ys[k]).then_inc(stored[k], 16)

                pipelined(sp, body, LATE, N, N + LATE, LOADS)
                for st in stored:
                    sp.wait_ge(st, 16 * (N // 2))

            if pool_job is not None:
                block.gpsimd(pool_job)

            @block.tensor
            def _(pe):
                if routing is not None:
                    routing.count(pe)
                    pe.wait_ge(routing.done, PICKED + 1)
                    pe.wait_ge(routing.copied, 1)
                cols = [None]

                def body(t, v):
                    one, two, three = stages(t)
                    u = v % 2
                    if v == 0:
                        _, cols[0] = nc.values_load_multi_w_load_instructions(
                            self.tile_cols[half][0:1, bass.ds(t, 5)], engines=[nc.tensor.engine],
                            min_val=0, max_val=(EXPERTS - 1) * HIDDEN,
                            skip_runtime_bounds_check_because="route() clamps them")
                    e_new, e_old = cols[0][v + 1], cols[0][v]
                    if one:
                        pe.wait_ge(loaded[v], 4 * (t - v) + 16)
                        at_least(pe, xT_ready, 2 * t)
                        pe.transpose(PS[:, XT_BANK, 0:P], xs[v], self.ident).then_inc(xT_done, 1)
                    if three:
                        i = t - 2
                        pe.wait_ge(h_ready, i + 1)
                        at_least(pe, hT_ready, i - 1)
                        for c in range(CHUNKS):
                            mm = pe.transpose(PS[:, HT_BANK + u, c * P:(c + 1) * P],
                                              hid[u][:, c * P:(c + 1) * P], self.ident)
                        mm.then_inc(hT_done, 1)
                    if two:
                        i = t - 1
                        pe.wait_ge(xT_ready, 2 * i + 2)
                        for w, bank, free, done in ((w_gate, GATE_BANK, silu_ready, gate_done),
                                                    (w_up, UP_BANK, h_ready, up_done)):
                            at_least(pe, free, i - 1)
                            for n, (a, b) in enumerate(((1, 0), (0, 1), (0, 0))):
                                mm = pe.matmul(PS[:, bank + 1 - u, :], xT[1 - u][a],
                                               w[b][:, bass.ds(e_new, HIDDEN)],
                                               start=(n == 0), stop=(n == 2))
                            mm.then_inc(done, 1)
                    if three:
                        pe.wait_ge(hT_ready, t - 1)
                        at_least(pe, y_ready, t - 2)
                        for c in range(CHUNKS):
                            mm = pe.matmul(PS[:, Y_BANK, 0:D], hT[u][:, c * P:(c + 1) * P],
                                           self.w_down[:, bass.ds(e_old + c * D, D)],
                                           start=(c == 0), stop=(c == CHUNKS - 1))
                        mm.then_inc(y_done, 1)

                pipelined(pe, body, 4, N, N + 2, 4)

            @block.scalar
            def _(act):
                if routing is not None:
                    routing.exponential(act)

                def body(t, u):
                    one, two, three = stages(t)
                    if three:
                        i = t - 2
                        act.wait_ge(hT_done, i + 1)
                        act.activation(hT[u], PS[:, HT_BANK + u, :], ACT.Copy).then_inc(hT_ready, 1)
                    if two:
                        i = t - 1
                        act.wait_ge(gate_done, i + 1)
                        act.activation(sg[1 - u], PS[:, GATE_BANK + 1 - u, :], ACT.Silu)\
                           .then_inc(silu_ready, 1)

                pipelined(act, body, 4, N, N + 2, 2)

            @block.vector
            def _(dve):
                if routing is not None:
                    for stage in routing.stages[:BEFORE]:
                        stage(dve)

                def body(t, u):
                    one, two, three = stages(t)
                    if one:
                        dve.wait_ge(xT_done, t + 1)
                        dve.tensor_copy(xT[u][0], PS[:, XT_BANK, 0:P]).then_inc(xT_ready, 1)
                        dve.wait_ge(xT_ready, 2 * t + 1)
                        dve.tensor_tensor(xT[u][1], PS[:, XT_BANK, 0:P], xT[u][0].bitcast(F32),
                                          ALU.subtract).then_inc(xT_ready, 1)
                    if two:
                        i = t - 1
                        dve.wait_ge(silu_ready, i + 1)
                        dve.wait_ge(up_done, i + 1)
                        dve.tensor_tensor(hid[1 - u], PS[:, UP_BANK + 1 - u, :], sg[1 - u], ALU.mult)\
                           .then_inc(h_ready, 1)
                    if three:
                        i = t - 2
                        at_least(dve, stored[u], 8 * (t - u) - 16 if not isinstance(t, int) else 16 * (i // 2))
                        dve.wait_ge(y_done, i + 1)
                        dve.tensor_copy(ys[u], PS[:, Y_BANK, 0:D]).then_inc(y_ready, 1)

                def routed(t, u):
                    body(t, u)
                    if routing is not None and isinstance(t, int) and BEFORE + t < len(routing.stages):
                        routing.stages[BEFORE + t](dve)

                pipelined(dve, routed, 8, N, N + 2, 2)

    def combine(self, tag, half):
        nc = self.nc
        DEEP = 8
        gathered = [self.sem(f"{tag}_c_gathered{i}") for i in range(DEEP)]
        half_done, x_done, out_done = (self.sem(f"{tag}_c_{n}") for n in ("half_done", "x_done", "out_done"))
        y = [[self.scratch[:, (2 * i + k) * D:(2 * i + k + 1) * D] for k in range(2)] for i in range(DEEP)]
        first = half * H_TILES
        with nc.Block() as block:
            @block.gpsimd
            def _(pool):
                for n in range(H_TILES):
                    t = first + n
                    at_least(pool, x_done, n - DEEP + 1)
                    for k in range(2):
                        pool.indirect_dma_start(
                            y[n % DEEP][k], None, self.y_slots[half],
                            bass.IndirectOffsetOnAxis(ap=self.slot[k][:, t:t + 1], axis=0))\
                            .then_inc(gathered[n % DEEP], 16)

            @block.vector
            def _(dve):
                for n in range(H_TILES):
                    t = first + n
                    dve.wait_ge(gathered[n % DEEP], 32 * (n // DEEP + 1))
                    for k, step in enumerate((half_done, x_done)):
                        dve.scalar_tensor_tensor(out=self.X[:, t, :], in0=y[n % DEEP][k],
                                                 scalar=self.gate[k][:, t:t + 1], in1=self.X[:, t, :],
                                                 op0=ALU.mult, op1=ALU.add).then_inc(step, 1)
                        if k == 0:
                            dve.wait_ge(half_done, n + 1)

            @block.sync
            def _(sp):
                out = self.dram["out"].rearrange("(t p) d -> p t d", p=P)
                sp.dma_start(out[:, 0:first, :], self.X[:, 0:first, :]).then_inc(out_done, 16)
                for i in range(ROUNDS):
                    sp.wait_ge(x_done, QUAD * (i + 1))
                    t = slice(first + QUAD * i, first + QUAD * (i + 1))
                    sp.dma_start(out[:, t, :], self.X[:, t, :]).then_inc(out_done, 16)
                sp.wait_ge(out_done, 16 * (ROUNDS + 1))


def build(nc, dram):
    with ExitStack() as ctx:
        k = Hybrid(nc, ctx, dram)
        k.setup()

        def all_tiles(step):
            def job(pool):
                for n in range(H_TILES):
                    step(pool, n)
            return job

        def every_other(step):
            def between(pool, s):
                if s % 2:
                    step(pool, s // 2)
            return between

        def from_step(first, step):
            def between(pool, s):
                if first <= s < first + H_TILES:
                    step(pool, s - first)
            return between

        for layer, causal in (("a", False), ("b", True)):
            loads, between = k.weights() if layer == "a" else \
                (None, every_other(k.gather("a1", 1, k.y_rows)))
            k.project(f"{layer}0", 0, causal, k.tables if layer == "a" else None)
            k.attend(f"{layer}0_s", 0, causal, between, loads)
            k.finish(f"{layer}0", 0)
            k.project(f"{layer}1", 1, causal)
            routing = Routing(k, f"{layer}0", 0, k.PS[:, 6, :])
            k.attend(f"{layer}1_s", 1, causal, from_step(12, k.scatter(f"{layer}0", 0, routing)),
                     routing=routing)
            k.finish(f"{layer}1", 1)
            routing = Routing(k, f"{layer}1", 1, k.PS[:, 6, :])
            k.experts(f"{layer}0", 0, all_tiles(k.scatter(f"{layer}1", 1, routing)), routing)
            k.experts(f"{layer}1", 1, all_tiles(k.gather(f"{layer}0", 0, k.y_rows)))
            if layer == "a":
                k.fresh_semaphores()
        k.combine("b1", 1)


def constants():
    p = np.arange(P)
    keep = np.zeros((P, C_KEEP), np.float32)
    keep[:, C_IDENT:C_IDENT + P] = np.eye(P)
    keep[:, C_TRI:C_TRI + P] = p[:, None] < p[None, :]
    freqs = np.float32(THETA) ** (-np.arange(0, DH, 2, dtype=np.float32) / np.float32(DH))
    angle = np.arange(S, dtype=np.float32)[None, :] * freqs[(p % DH) // 2][:, None]
    keep[:, C_COS:C_COS + S] = np.cos(angle)
    keep[:, C_SIN:C_SIN + S] = np.sin(angle) * np.where(p % 2 == 0, -1, 1)[:, None]
    keep[:, C_KBIAS] = p % ROW == SHIFT_ROW
    keep[:, C_RANK:C_RANK + EXPERTS] = EXPERTS - np.arange(EXPERTS)
    keep[:, C_START:C_START + SLOT_TILES] = np.arange(SLOT_TILES) * P
    key_mask = np.zeros((P, 2 * P), np.float32)
    perm = np.zeros((P, N_PERM), np.float32)
    keep[:, C_QMASK + P:C_QMASK + 2 * P] = np.where(p[None, :] > p[:, None], MASKED, 0)
    for a in range(2):
        key_mask[:, a * P:(a + 1) * P] = np.where(p[:, None] > p[None, :], MASKED, 0)
    for n, blocks in enumerate(((0, 1), (2,), (0, 2), (1,))):
        for g in range(GROUPS):
            for j in range(QUAD):
                for b in blocks:
                    for d in range(DH):
                        perm[DH * (QUAD * g + j) + d, (n * GROUPS + g) * P + ROW * j + DH * b + d] = 1
    return keep, key_mask, perm


def kernel(**inputs):
    import concourse.bacc as _bacc
    from concourse.bass_utils import run_bass_kernel_spmd as _run

    a = {n: np.asarray(v) for n, v in inputs.items()}
    c = np.ascontiguousarray
    keep, key_mask, perm = constants()
    swap = np.arange(D) ^ 1
    A, Bn, Fn = "L0_attn_a_", "L0_attn_b_", "L0_ffn_"
    arrays = {
        "x": c(a[A + "x"].reshape(TOKENS, D)),
        "consts": keep, "key_mask": key_mask, "perm": perm,
        "w_a_q": c(a[A + "Wq"].T), "w_a_k": c(a[A + "Wk"].T), "w_a_v": c(a[A + "Wv"].T),
        "w_a_o": c(a[A + "Wff"].T),
        "w_b_q": c(a[Bn + "Wq"].T), "w_b_k": c(a[Bn + "Wk"].T), "w_b_v": c(a[Bn + "Wv"].T),
        "w_b_qs": c(a[Bn + "Wq"][swap].T), "w_b_ks": c(a[Bn + "Wk"][swap].T), "w_b_o": c(a[Bn + "Wo"].T),
        "bias_q": a[Bn + "bq"], "bias_k": a[Bn + "bk"], "bias_qs": c(a[Bn + "bq"][swap]),
        "bias_ks": c(a[Bn + "bk"][swap]), "bias_scale": a[Bn + "scale"],
        "rows_a_o": a[A + "bff"], "rows_b_v": a[Bn + "bv"], "rows_b_o": a[Bn + "bo"],
        "w_route": c(a[Fn + "wg"].T), "b_route": a[Fn + "bg"],
        "w_gate": c(a[Fn + "Wgate"].transpose(2, 0, 1).reshape(D, EXPERTS * HIDDEN)),
        "w_up": c(a[Fn + "Wup"].transpose(2, 0, 1).reshape(D, EXPERTS * HIDDEN)),
        "w_down": c(a[Fn + "Wdown"].reshape(EXPERTS, D, CHUNKS, P).transpose(3, 0, 2, 1)
                    .reshape(P, EXPERTS * CHUNKS * D)),
    }
    from concourse import mybir as _mybir
    nc = _bacc.Bacc("TRN2", target_bir_lowering=False, num_devices=1)
    dram = {n: nc.dram_tensor(f"in_{n}", v.shape, _mybir.dt.from_np(v.dtype), kind="ExternalInput").ap()
            for n, v in arrays.items()}
    dram["out"] = nc.dram_tensor("out", (TOKENS, D), F32, kind="ExternalOutput").ap()
    build(nc, dram)
    r = _run(nc, [{f"in_{n}": v for n, v in arrays.items()}], core_ids=[0])
    return r.results[0]["out"].reshape(B, S, D)
```
